# Optimizing a Trainium2 kernel written in Bass

```python
import numpy as np
import jax
import jax.numpy as jnp

def _softmax(x, axis=-1):
    return jax.nn.softmax(x, axis=axis)

def _gelu(x):
    return jax.nn.gelu(x, approximate=True)

def _silu(x):
    return jax.nn.silu(x)

def _sigmoid(x):
    return jax.nn.sigmoid(x)

def _layernorm(x, axis=-1, eps=1e-05):
    m = jnp.mean(x, axis=axis, keepdims=True)
    v = jnp.var(x, axis=axis, keepdims=True)
    return (x - m) / jnp.sqrt(v + eps)

def _scatter_add(tgt, idx, src, axis=0):
    return tgt.at[idx].add(src)

def _segment_sum(src, seg, n):
    return jax.ops.segment_sum(src, seg, n)
kernel_name = 'mk_gnn_resnorm_d1_gnn_r8_f559d2'

def setup_inputs(seed: int=0):
    np.random.seed(seed)
    _w = jnp.asarray

    def _rec_inputs():
        import jax
        import jax.numpy as jnp
        _gk = jax.random.key(seed)
        x = -0.0009044 + 1 * jax.random.normal(jax.random.fold_in(_gk, 1), (12500, 32), jnp.float32)
        src = jax.random.randint(jax.random.fold_in(_gk, 2), (200000,), 0, 12500, jnp.int32)
        dst = jnp.minimum((12500 * jax.random.uniform(jax.random.fold_in(_gk, 3), (200000,)) ** 2.0).astype(jnp.int32), 99999)
        _o = jnp.argsort(dst, stable=True)
        src = src[_o]
        dst = dst[_o]
        edge_type_86 = jax.random.randint(jax.random.fold_in(_gk, 12), (200000,), 0, 86, jnp.int32)
        return (x, src, dst, edge_type_86)
    x, src, dst, edge_type_86 = _rec_inputs()

    def _L0_gnn_setup():
        import jax, jax.numpy as jnp
        import numpy as np
        N_NODES = 6250
        N_EDGES = 100000
        INP_DIM = 32
        OUT_DIM = 32
        ATTN_DIM = 32
        NUM_RELS = 86
        NUM_BASES = 16
        GAMMA = 0.0
        key = jax.random.key(seed)
        ks = jax.random.split(key, 12)
        return {'h': jax.random.normal(ks[0], (N_NODES, INP_DIM), jnp.float32), 'weight': jax.random.normal(ks[1], (NUM_BASES, INP_DIM, OUT_DIM), jnp.float32), 'w_comp': jax.random.normal(ks[2], (NUM_RELS, NUM_BASES), jnp.float32), 'self_loop_weight': jax.random.normal(ks[3], (INP_DIM, OUT_DIM), jnp.float32), 'A1_w': jax.random.normal(ks[4], (ATTN_DIM, INP_DIM), jnp.float32), 'A1_b': jax.random.normal(ks[5], (ATTN_DIM,), jnp.float32), 'A2_w': jax.random.normal(ks[6], (ATTN_DIM, INP_DIM), jnp.float32), 'A2_b': jax.random.normal(ks[7], (ATTN_DIM,), jnp.float32), 'rel_emb': jax.random.normal(ks[8], (NUM_RELS, ATTN_DIM), jnp.float32), 'src': jax.random.randint(ks[9], (N_EDGES,), 0, N_NODES, jnp.int32), 'dst': jax.random.randint(ks[10], (N_EDGES,), 0, N_NODES, jnp.int32), 'etype': jax.random.randint(ks[11], (N_EDGES,), 0, NUM_RELS, jnp.int32)}
    _L0_gnn_all = _L0_gnn_setup()
    _L0_gnn_in = {k: v for k, v in _L0_gnn_all.items() if k in ('weight', 'w_comp', 'self_loop_weight', 'A1_w', 'A1_b', 'A2_w', 'A2_b', 'rel_emb')}
    del _L0_gnn_all
    return {'x': x, 'src': src, 'dst': dst, 'edge_type_86': edge_type_86, 'L0_gnn_weight': _L0_gnn_in['weight'], 'L0_gnn_w_comp': _L0_gnn_in['w_comp'], 'L0_gnn_self_loop_weight': _L0_gnn_in['self_loop_weight'], 'L0_gnn_A1_w': _L0_gnn_in['A1_w'], 'L0_gnn_A1_b': _L0_gnn_in['A1_b'], 'L0_gnn_A2_w': _L0_gnn_in['A2_w'], 'L0_gnn_A2_b': _L0_gnn_in['A2_b'], 'L0_gnn_rel_emb': _L0_gnn_in['rel_emb']}

def reference(x, src, dst, edge_type_86, L0_gnn_weight, L0_gnn_w_comp, L0_gnn_self_loop_weight, L0_gnn_A1_w, L0_gnn_A1_b, L0_gnn_A2_w, L0_gnn_A2_b, L0_gnn_rel_emb):
    import jax
    import jax.numpy as jnp

    def _L0_gnn_ref(h, weight, w_comp, self_loop_weight, A1_w, A1_b, A2_w, A2_b, rel_emb, src, dst, etype):
        import jax, jax.numpy as jnp
        import numpy as np
        N_NODES = 6250
        N_EDGES = 100000
        INP_DIM = 32
        OUT_DIM = 32
        ATTN_DIM = 32
        NUM_RELS = 86
        NUM_BASES = 16
        GAMMA = 0.0
        E = src.shape[0]
        N = h.shape[0]
        x = h[src]
        y = h[dst]
        c = w_comp[etype]
        xb = jnp.einsum('ei,bio->ebo', x, weight)
        msg = jnp.einsum('eb,ebo->eo', c, xb)
        x_hat = x @ A1_w.T + A1_b
        y_hat = y @ A2_w.T + A2_b + rel_emb[etype]
        scale = jnp.sqrt(jnp.asarray(INP_DIM, h.dtype))
        a = jnp.tanh(jax.nn.relu(jnp.sum(x_hat * y_hat, axis=-1) / scale))
        a = jnp.where(a > GAMMA, a, jnp.zeros_like(a))
        nei = jax.ops.segment_sum(a[:, None] * msg, dst, num_segments=N)
        last_e = jax.ops.segment_max(jnp.arange(E, dtype=jnp.int32), dst, num_segments=N)
        last_e = jnp.clip(last_e, 0, E - 1)
        curr = h[src[last_e]] @ self_loop_weight
        in_deg = jax.ops.segment_sum(jnp.ones((E,), h.dtype), dst, num_segments=N)
        h_new = jnp.where((in_deg > 0)[:, None], nei + curr, jnp.zeros_like(nei))
        return jax.nn.relu(h_new)
    x = _layernorm(x + _L0_gnn_ref(x, L0_gnn_weight, L0_gnn_w_comp, L0_gnn_self_loop_weight, L0_gnn_A1_w, L0_gnn_A1_b, L0_gnn_A2_w, L0_gnn_A2_b, L0_gnn_rel_emb, src, dst, edge_type_86), axis=-1)
    return x

_drawn_inputs = setup_inputs


def setup_inputs(seed=0):
    import zlib

    import numpy as np

    out = dict(_drawn_inputs(seed))
    spreads = {}
    factors = {}
    for name, (base, spread) in spreads.items():
        noise = np.random.default_rng([zlib.crc32(name.encode()), seed]).standard_normal(out[name].shape)
        drawn = base * np.exp(spread * noise) if base else spread * noise
        out[name] = jnp.asarray(drawn.astype(out[name].dtype))
    for name, factor in factors.items():
        out[name] = (out[name] * factor).astype(out[name].dtype)
    return out
```

```python
from contextlib import ExitStack

import concourse.bass as bass
from concourse import mybir

F32 = mybir.dt.float32
BF16 = mybir.dt.bfloat16
I32 = mybir.dt.int32
ALU = mybir.AluOpType
ACT = mybir.ActivationFunctionType
AX_X = mybir.AxisListType.X


def build(nc, x, src, dst, etype, weight, w_comp, w_self, a1_w, a1_b, a2_w, a2_b, rel_emb, out):
    N, D = x.shape
    E = src.shape[0]
    R, NB = w_comp.shape
    P = 128
    NP_ = 125
    NT = N // NP_
    D1 = D + 1
    TW = NB + D1
    UW = (NB + 1) * D
    KB = NB * D // P
    BPK = NB // KB
    ROWS = N + P
    NF = ROWS

    GC = 125
    GN = E // GC
    QB = 4
    HB = 10

    q_dram = nc.dram_tensor("q_table", (ROWS, 3 * D1), BF16).ap()
    rt_dram = nc.dram_tensor("rel_table", (R, 3 * TW), BF16).ap()
    z_dram = nc.dram_tensor("z_rows", (ROWS, UW), F32).ap()

    with ExitStack() as ctx:
        def sb(name, shape, dt):
            return ctx.enter_context(nc.sbuf_tensor(name, shape, dt))

        def psum(name, shape, dt):
            return ctx.enter_context(nc.psum_tensor(name, shape, dt))

        def sem(name):
            return ctx.enter_context(nc.semaphore(name))

        ident = sb("ident", [P, P], F32)
        iota_pi = sb("iota_pi", [P, 1], I32)
        iota_ri = sb("iota_ri", [P, P], I32)
        iota_p = sb("iota_p", [P, 1], F32)
        iota_r = sb("iota_r", [P, P], F32)
        upper = sb("upper", [P, P], F32)
        trash = sb("trash", [P, 1], F32)
        xr = sb("xr", [NP_, NT * D], F32)
        a1 = sb("a1", [D, D1], F32)
        a2 = sb("a2", [D, D1], F32)
        rel = sb("rel", [R, D], F32)
        relT = sb("relT", [D, R], F32)
        bmat = sb("bmat", [D1, D1], F32)
        wf = sb("wf", [P, KB, D], F32)
        ws = sb("ws", [D, D], F32)
        xT = sb("xT", [D1, 2, QB * NP_], F32)
        rtf = sb("rtf", [R, TW], F32)
        rtr = sb("rtr", [R, TW], F32)
        rt3 = sb("rt3", [R, 3, TW], BF16)
        qf = sb("qf", [NP_, NT, D1], F32)
        qr = sb("qr", [NP_, NT, D1], F32)
        q3 = sb("q3", [NP_, NT, 3, D1], BF16)
        zero = sb("zero", [P, 2 * UW], F32)
        accT = sb("accT", [D, NF], F32)

        g_idx = sb("g_idx", [GC, 3], I32)
        g_sidx = sb("g_sidx", [GC, 1], I32)
        g_row = sb("g_row", [GC, GC], I32)
        g_x = sb("g_x", [GC, D1], F32)
        g_q = sb("g_q", [GC, 3 * D1], BF16)
        g_rt = sb("g_rt", [GC, 3 * TW], BF16)
        g_z = sb("g_z", [GC, UW], F32)
        g_v = sb("g_v", [GC, D1], F32)
        g_c = sb("g_c", [GC, TW], F32)
        g_sc = sb("g_sc", [GC, 4], F32)
        g_w = sb("g_w", [GC, NB + 1], F32)
        g_same = sb("g_same", [GC, GC], F32)
        g_later = sb("g_later", [GC, GC], F32)
        g_u = sb("g_u", [GC, UW], F32)
        g_new = sb("g_new", [GC, UW], F32)
        f_z = sb("f_z", [GC, UW], F32)
        f_zT = sb("f_zT", [P, KB + 1, GC], F32)
        y = sb("y", [NP_, NT, D], F32)
        ysq = sb("ysq", [NP_, NT, D], F32)
        mean = sb("mean", [NP_, NT], F32)
        var = sb("var", [NP_, NT], F32)

        ps = [psum(f"ps{i}", [P, 512], F32) for i in range(8)]

        s_load = sem("s_load")
        s_x = sem("s_x")
        s_pool = sem("s_pool")
        s_const = sem("s_const")
        s_pe = sem("s_pe")
        s_bm = sem("s_bm")
        s_xT = sem("s_xT")
        s_xTs = sem("s_xTs")
        s_q = sem("s_q")
        s_qf = sem("s_qf")
        s_spl = sem("s_spl")
        s_tab = sem("s_tab")
        g_loaded = [sem(f"g_loaded{k}") for k in range(4)]
        g_zeroed = sem("g_zeroed")
        g_done = sem("g_done")
        g_turn = sem("g_turn")
        g_gathered = [sem(f"g_gathered{k}") for k in range(4)]
        g_vec = sem("g_vec")
        g_tanh = sem("g_tanh")
        g_summed = sem("g_summed")
        g_scattered = sem("g_scattered")
        f_loaded = sem("f_loaded")
        f_turned = sem("f_turned")
        f_copied = sem("f_copied")
        f_summed = sem("f_summed")
        f_stored = sem("f_stored")
        h_turned = sem("h_turned")
        h_vec = sem("h_vec")
        h_std = sem("h_std")
        s_out = sem("s_out")

        block = ctx.enter_context(nc.Block())
        NBATCH = NT // QB
        GV = 17

        @block.sync
        def _(sp):
            sp.dma_start(xr[:], x.rearrange("(p t) d -> p (t d)", t=NT)).then_inc(s_x, 16)
            sp.dma_start(a1[:, 0:D], a1_w).then_inc(s_load, 16)
            sp.dma_start(a1[:, D:D1], a1_b.rearrange("(a b) -> a b", b=1)).then_inc(s_load, 16)
            sp.dma_start(a2[:, 0:D], a2_w).then_inc(s_load, 16)
            sp.dma_start(a2[:, D:D1], a2_b.rearrange("(a b) -> a b", b=1)).then_inc(s_load, 16)
            sp.dma_start(rel[:], rel_emb).then_inc(s_load, 16)
            sp.dma_start(rtf[:, 0:NB], w_comp).then_inc(s_load, 16)
            sp.dma_start(wf[:], weight.rearrange("(k b) i o -> (b i) k o", k=KB)).then_inc(s_load, 16)
            sp.dma_start(ws[:], w_self).then_inc(s_load, 16)
            sp.wait_ge(s_spl, 10)
            sp.dma_start(q_dram[0:N, :].rearrange("(p t) c -> p (t c)", t=NT), q3[:].rearrange("p t a c -> p (t a c)")).then_inc(s_tab, 16)
            sp.dma_start(rt_dram[:, :], rt3[:].rearrange("r a c -> r (a c)")).then_inc(s_tab, 16)
            sp.wait_ge(s_pool, 1)
            sp.dma_start(q_dram[N:ROWS, :], zero[:].bitcast(BF16)[:, 0:3 * D1]).then_inc(s_tab, 16)
            sp.dma_start(z_dram[0:P, :], zero[:, 0:UW]).then_inc(g_zeroed, 16)
            for k in range(N // (2 * GC)):
                sp.dma_start(z_dram[P + k * 250:P + (k + 1) * 250, :].rearrange("(p r) c -> p (r c)", r=2), zero[0:GC, :]).then_inc(g_zeroed, 16)
            Z0 = N // (2 * GC) + 1
            sp.wait_ge(s_tab, 48)
            sp.wait_ge(g_zeroed, Z0 * 16)
            with sp.Fori(0, GN) as i:
                sp.dma_start(g_idx[:, 0:1], src[bass.ds(i * GC, GC)].rearrange("(a b) -> a b", b=1)).then_inc(g_loaded[0], 16)
                sp.dma_start(g_idx[:, 1:2], dst[bass.ds(i * GC, GC)].rearrange("(a b) -> a b", b=1)).then_inc(g_loaded[1], 16)
                sp.dma_start(g_idx[:, 2:3], etype[bass.ds(i * GC, GC)].rearrange("(a b) -> a b", b=1)).then_inc(g_loaded[2], 16)
                sp.dma_start(g_row[:], dst[bass.ds(i * GC, GC)].rearrange("(a b) -> a b", a=1).broadcast_to([GC, GC])).then_inc(g_loaded[3], 16)
                sp.wait_ge(g_scattered, i * 16 + 16).then_inc(g_done, 1)
            with sp.Fori(0, NT) as t:
                sp.wait_ge(f_stored, t + 1)
                sp.dma_start(f_z[:], z_dram[bass.ds(t * GC, GC), :]).then_inc(f_loaded, 16)
            sp.wait_ge(h_vec, 16)
            sp.dma_start(out.rearrange("(p t) d -> p (t d)", t=NT), ysq[:].rearrange("p t d -> p (t d)")).then_inc(s_out, 16)
            sp.wait_ge(s_out, 16)

        @block.gpsimd
        def _(pool):
            nc.gpsimd.memset(zero[:], 0.0).then_inc(s_pool, 1)
            nc.gpsimd.memset(ident[:], 0.0).then_inc(s_pool, 1)
            nc.gpsimd.iota(iota_pi[:], pattern=[[0, 1]], base=0, channel_multiplier=1).then_inc(s_pool, 1)
            nc.gpsimd.iota(iota_ri[:], pattern=[[1, P]], base=0, channel_multiplier=0).then_inc(s_pool, 1)
            pool.wait_ge(s_pool, 2)
            nc.gpsimd.affine_select(out=ident[:], in_=ident[:], compare_op=ALU.not_equal, fill=1.0, base=0,
                                    pattern=[[-1, P]], channel_multiplier=1).then_inc(s_pool, 1)
            pool.wait_ge(s_tab, 48)
            with pool.Fori(0, GN) as i:
                for k in range(4):
                    pool.wait_ge(g_loaded[k], i * 16 + 16).then_inc(g_turn, 1)
                nc.gpsimd.indirect_dma_start(g_x[:, 0:D], None, x, bass.IndirectOffsetOnAxis(ap=g_idx[:, 0:1], axis=0)).then_inc(g_gathered[0], 16)
                nc.gpsimd.indirect_dma_start(g_q[:], None, q_dram, bass.IndirectOffsetOnAxis(ap=g_idx[:, 1:2], axis=0)).then_inc(g_gathered[1], 16)
                nc.gpsimd.indirect_dma_start(g_rt[:], None, rt_dram, bass.IndirectOffsetOnAxis(ap=g_idx[:, 2:3], axis=0)).then_inc(g_gathered[2], 16)
                nc.gpsimd.indirect_dma_start(g_z[:], None, z_dram, bass.IndirectOffsetOnAxis(ap=g_idx[:, 1:2], axis=0)).then_inc(g_gathered[3], 16)
                pool.wait_ge(g_vec, i * GV + GV).then_inc(g_turn, 1)
                nc.gpsimd.indirect_dma_start(z_dram, bass.IndirectOffsetOnAxis(ap=g_sidx[:], axis=0), g_new[:], None).then_inc(g_scattered, 16)

        @block.scalar
        def _(act):
            for b in range(NBATCH):
                act.wait_ge(s_xT, b + 1)
                if b >= 2:
                    act.wait_ge(s_q, b - 1)
                nc.scalar.copy(xT[0:D, b % 2, :], ps[b % 2][0:D, 0:QB * NP_]).then_inc(s_xTs, 1)
            with act.Fori(0, GN) as i:
                act.wait_ge(g_vec, i * GV + 8)
                nc.scalar.activation(g_sc[:, 1:2], g_sc[:, 0:1], ACT.Tanh, scale=float(D) ** -0.5).then_inc(g_tanh, 1)
            with act.Fori(0, NT) as t:
                act.wait_ge(f_turned, t + 1)
                act.wait_ge(f_summed, t + 1)
                nc.scalar.copy(f_zT[:, 0:KB, :].rearrange("p k n -> p (k n)"), ps[0][:, 0:KB * GC]).then_inc(f_copied, 1)
                nc.scalar.copy(f_zT[0:D, KB, :], ps[1][0:D, 0:GC]).then_inc(f_copied, 1)
            act.wait_ge(h_vec, 13)
            nc.scalar.activation(mean[:], var[:], ACT.Sqrt).then_inc(h_std, 1)

        def pe_q(pe, b):
            pe.wait_ge(s_xTs, b + 1)
            if b >= 2:
                pe.wait_ge(s_qf, b - 1)
            for j in range(QB):
                last = nc.tensor.matmul(ps[2 + b % 2][0:NP_, j * D1:(j + 1) * D1], xT[:, b % 2, j * NP_:(j + 1) * NP_], bmat[:], start=True, stop=True)
            last.then_inc(s_q, 1)

        @block.tensor
        def _(pe):
            pe.wait_ge(s_pool, 5)
            pe.wait_ge(s_load, 128)
            nc.tensor.transpose(ps[4][0:D, 0:R], rel[:], ident[0:R, 0:R]).then_inc(s_pe, 1)
            nc.tensor.matmul(ps[5][0:D1, 0:D1], a2[:], a1[:], start=True, stop=True).then_inc(s_pe, 1)
            pe.wait_ge(s_bm, 1)
            nc.tensor.matmul(ps[6][0:R, 0:D1], relT[:], a1[:], start=True, stop=True).then_inc(s_pe, 1)
            pe.wait_ge(s_x, 16)
            pe.wait_ge(s_bm, 3)
            for b in range(NBATCH):
                if b >= 2:
                    pe.wait_ge(s_xTs, b - 1)
                for j in range(QB):
                    t = b * QB + j
                    last = nc.tensor.transpose(ps[b % 2][0:D, j * NP_:(j + 1) * NP_], xr[:, t * D:(t + 1) * D], ident[0:NP_, 0:NP_])
                last.then_inc(s_xT, 1)
                if b >= 1:
                    pe_q(pe, b - 1)
            pe_q(pe, NBATCH - 1)
            with pe.Fori(0, GN) as i:
                pe.wait_ge(g_vec, i * GV + 15)
                for h in range(2):
                    last = nc.tensor.matmul(ps[h][0:GC, 0:UW // 2], g_same[:], g_u[:, h * (UW // 2):(h + 1) * (UW // 2)], start=True, stop=True)
                last.then_inc(g_summed, 1)
            with pe.Fori(0, NT) as t:
                pe.wait_ge(f_loaded, t * 16 + 16)
                pe.wait_ge(f_stored, t + 1)
                for k in range(KB):
                    nc.tensor.transpose(ps[0][:, k * GC:(k + 1) * GC], f_z[:, k * P:(k + 1) * P], ident[0:GC, 0:GC])
                nc.tensor.transpose(ps[1][0:D, 0:GC], f_z[:, KB * P:UW], ident[0:GC, 0:GC]).then_inc(f_turned, 1)
                pe.wait_ge(f_copied, t * 2 + 2)
                for k in range(KB):
                    nc.tensor.matmul(ps[2][0:D, 0:GC], wf[:, k, :], f_zT[:, k, :], start=(k == 0), stop=False)
                nc.tensor.matmul(ps[2][0:D, 0:GC], ws[:], f_zT[0:D, KB, :], start=False, stop=True).then_inc(f_summed, 1)
            pe.wait_ge(f_stored, NT + 1)
            for b in range(NT // HB):
                if b >= 4:
                    pe.wait_ge(h_vec, b - 3)
                for j in range(HB):
                    t = b * HB + j
                    last = nc.tensor.transpose(ps[b % 4][0:NP_, j * D:(j + 1) * D], accT[:, t:N:NT], ident[0:D, 0:D])
                last.then_inc(h_turned, 1)

        @block.vector
        def _(dve):
            nc.vector.memset(xT[D:D1, :, :], 1.0).then_inc(s_const, 1)
            nc.vector.memset(g_x[:, D:D1], 1.0).then_inc(s_const, 1)
            dve.wait_ge(s_pool, 4)
            nc.vector.tensor_copy(iota_p[:], iota_pi[:]).then_inc(s_const, 1)
            nc.vector.tensor_copy(iota_r[:], iota_ri[:]).then_inc(s_const, 1)
            dve.wait_ge(s_const, 4)
            nc.vector.tensor_scalar(upper[:], iota_r[:], iota_p[:, 0:1], None, ALU.is_gt).then_inc(s_const, 1)
            nc.vector.tensor_scalar(trash[:], iota_p[:], float(N), None, ALU.add).then_inc(s_const, 1)
            dve.wait_ge(s_pe, 1)
            nc.vector.tensor_copy(relT[:], ps[4][0:D, 0:R]).then_inc(s_bm, 1)
            dve.wait_ge(s_pe, 2)
            nc.vector.tensor_copy(bmat[:], ps[5][0:D1, 0:D1]).then_inc(s_bm, 1)
            dve.wait_ge(s_pe, 3)
            nc.vector.tensor_copy(rtf[:, NB:TW], ps[6][0:R, 0:D1]).then_inc(s_bm, 1)
            for b in range(NBATCH):
                dve.wait_ge(s_q, b + 1)
                nc.vector.tensor_copy(qf[:, b * QB:(b + 1) * QB, :].rearrange("p t c -> p (t c)"), ps[2 + b % 2][0:NP_, 0:QB * D1]).then_inc(s_qf, 1)
            dve.wait_ge(s_bm, 3)
            dve.wait_ge(s_qf, NBATCH)
            n = 0
            for full, rest, parts in ((rtf, rtr, [rt3[:, a, :] for a in range(3)]), (qf, qr, [q3[:, :, a, :] for a in range(3)])):
                nc.vector.tensor_copy(parts[0], full[:]).then_inc(s_spl, 1)
                dve.wait_ge(s_spl, n + 1)
                nc.vector.tensor_tensor(rest[:], full[:], parts[0], ALU.subtract).then_inc(s_spl, 1)
                dve.wait_ge(s_spl, n + 2)
                nc.vector.tensor_copy(parts[1], rest[:]).then_inc(s_spl, 1)
                dve.wait_ge(s_spl, n + 3)
                nc.vector.tensor_tensor(full[:], rest[:], parts[1], ALU.subtract).then_inc(s_spl, 1)
                dve.wait_ge(s_spl, n + 4)
                nc.vector.tensor_copy(parts[2], full[:]).then_inc(s_spl, 1)
                n += 5
            dve.wait_ge(s_const, 6)
            with dve.Fori(0, GN) as i:
                for k in range(4):
                    dve.wait_ge(g_gathered[k], i * 16 + 16)
                n = [0]

                def step(ins, wait=True):
                    n[0] += 1
                    ins.then_inc(g_vec, 1)
                    if wait:
                        dve.wait_ge(g_vec, i * GV + n[0])
                step(nc.vector.tensor_tensor(g_v[:], g_q[:, 0:D1], g_q[:, D1:2 * D1], ALU.add))
                step(nc.vector.tensor_tensor(g_v[:], g_v[:], g_q[:, 2 * D1:3 * D1], ALU.add))
                step(nc.vector.tensor_tensor(g_c[:], g_rt[:, 0:TW], g_rt[:, TW:2 * TW], ALU.add))
                step(nc.vector.tensor_tensor(g_c[:], g_c[:], g_rt[:, 2 * TW:3 * TW], ALU.add))
                step(nc.vector.tensor_tensor(g_v[:], g_v[:], g_c[:, NB:TW], ALU.add))
                step(nc.vector.tensor_tensor(g_v[:], g_v[:], g_x[:], ALU.mult))
                step(nc.vector.tensor_copy(g_sc[:, 2:3], g_idx[:, 1:2]))
                step(nc.vector.tensor_reduce(g_sc[:, 0:1], g_v[:], AX_X, ALU.add))
                step(nc.vector.tensor_scalar(g_same[:], g_row[:], g_sc[:, 2:3], None, ALU.is_equal))
                step(nc.vector.tensor_tensor(g_later[:], g_same[:], upper[0:GC, 0:GC], ALU.mult))
                step(nc.vector.tensor_reduce(g_sc[:, 3:4], g_later[:], AX_X, ALU.add))
                step(nc.vector.tensor_scalar(g_w[:, NB:NB + 1], g_sc[:, 3:4], 0.0, None, ALU.is_equal))
                dve.wait_ge(g_tanh, i + 1)
                step(nc.vector.scalar_tensor_tensor(out=g_w[:, 0:NB], in0=g_sc[:, 1:2].broadcast_to([GC, NB]), scalar=0.0, in1=g_c[:, 0:NB], op0=ALU.max, op1=ALU.mult))
                step(nc.vector.tensor_scalar(g_sc[:, 2:3], g_sc[:, 2:3], trash[0:GC, 0:1], g_w[:, NB:NB + 1], ALU.subtract, ALU.mult))
                step(nc.vector.tensor_tensor(g_u[:].rearrange("p (b d) -> p b d", d=D),
                                             g_w[:].rearrange("p (b o) -> p b o", o=1).broadcast_to([GC, NB + 1, D]),
                                             g_x[:, 0:D].rearrange("p (o d) -> p o d", o=1).broadcast_to([GC, NB + 1, D]), ALU.mult))
                step(nc.vector.tensor_scalar(g_sidx[:], g_sc[:, 2:3], trash[0:GC, 0:1], None, ALU.add), wait=False)
                dve.wait_ge(g_summed, i + 1)
                h = UW // 2
                nc.vector.tensor_tensor(g_new[:, 0:h], ps[0][0:GC, 0:h], g_z[:, 0:h], ALU.add)
                nc.vector.tensor_tensor(g_new[:, h:NB * D], ps[1][0:GC, 0:NB * D - h], g_z[:, h:NB * D], ALU.add)
                nc.vector.tensor_copy(g_new[:, NB * D:UW], ps[1][0:GC, NB * D - h:h]).then_inc(g_vec, 1)
            nc.vector.memset(accT[:, 0:1], 0.0).then_inc(f_stored, 1)
            nc.vector.memset(f_zT[0:D, KB, :], 0.0).then_inc(f_summed, 1)
            with dve.Fori(0, NT) as t:
                dve.wait_ge(f_summed, t + 2)
                nc.vector.tensor_copy(accT[:, bass.ds(t * GC, GC)], ps[2][0:D, 0:GC]).then_inc(f_stored, 1)
            for b in range(NT // HB):
                dve.wait_ge(h_turned, b + 1)
                nc.vector.scalar_tensor_tensor(out=y[:, b * HB:(b + 1) * HB, :].rearrange("p t d -> p (t d)"), in0=ps[b % 4][0:NP_, 0:HB * D],
                                               scalar=0.0, in1=xr[:, b * HB * D:(b + 1) * HB * D], op0=ALU.max, op1=ALU.add).then_inc(h_vec, 1)
            bc = [NP_, NT, D]
            dve.wait_ge(h_vec, 10)
            nc.vector.tensor_reduce(mean[:], y[:], AX_X, ALU.add).then_inc(h_vec, 1)
            dve.wait_ge(h_vec, 11)
            nc.vector.scalar_tensor_tensor(out=y[:], in0=mean[:].rearrange("p (t o) -> p t o", o=1).broadcast_to(bc), scalar=-1.0 / D, in1=y[:],
                                           op0=ALU.mult, op1=ALU.add).then_inc(h_vec, 1)
            dve.wait_ge(h_vec, 12)
            nc.vector.tensor_tensor(ysq[:], y[:], y[:], ALU.mult).then_inc(s_bm, 1)
            dve.wait_ge(s_bm, 4)
            nc.vector.tensor_reduce(var[:], ysq[:], AX_X, ALU.add).then_inc(s_bm, 1)
            dve.wait_ge(s_bm, 5)
            nc.vector.tensor_scalar(var[:], var[:], 1.0 / D, 1e-5, ALU.mult, ALU.add).then_inc(h_vec, 1)
            dve.wait_ge(h_std, 1)
            nc.vector.reciprocal(var[:], mean[:]).then_inc(h_vec, 1)
            dve.wait_ge(h_vec, 14)
            nc.vector.tensor_tensor(ysq[:], y[:], var[:].rearrange("p (t o) -> p t o", o=1).broadcast_to(bc), ALU.mult).then_inc(h_vec, 2)


_INS = ["x", "src", "dst", "edge_type_86", "L0_gnn_weight", "L0_gnn_w_comp", "L0_gnn_self_loop_weight",
        "L0_gnn_A1_w", "L0_gnn_A1_b", "L0_gnn_A2_w", "L0_gnn_A2_b", "L0_gnn_rel_emb"]


def kernel(**inputs):
    import numpy as _np
    import concourse.bacc as _bacc
    from concourse import mybir as _mybir
    from concourse.bass_utils import run_bass_kernel_spmd as _run

    nc = _bacc.Bacc("TRN2", target_bir_lowering=False, num_devices=1)
    arrays, args = {}, []
    for name in _INS:
        a = _np.ascontiguousarray(inputs[name])
        arrays[f"in_{name}"] = a
        args.append(nc.dram_tensor(f"in_{name}", a.shape, _mybir.dt.from_np(a.dtype), kind="ExternalInput").ap())
    out = nc.dram_tensor("out", args[0].shape, F32, kind="ExternalOutput").ap()
    build(nc, *args, out)
    r = _run(nc, [arrays], core_ids=[0])
    return r.results[0]["out"]
```

```python
from contextlib import ExitStack

import concourse.bass as bass
from concourse import mybir

F32 = mybir.dt.float32
BF16 = mybir.dt.bfloat16
I32 = mybir.dt.int32
ALU = mybir.AluOpType
ACT = mybir.ActivationFunctionType
AX_X = mybir.AxisListType.X


def build(nc, x, src, dst, etype, weight, w_comp, w_self, a1_w, a1_b, a2_w, a2_b, rel_emb, out):
    P = 128
    N, D = x.shape
    E = src.shape[0]
    R, NB = w_comp.shape
    D1 = D + 1
    CK = NB + D1
    UW = (NB + 1) * D
    HALF = UW // 2
    KB = NB * D // P
    ROWS = N + P
    SCALE = float(D) ** -0.5
    EPS = 1e-5
    HP = 32

    NPART = 125
    NT = N // NPART
    QB = 4
    NQ = NT // QB
    HB = 10
    NH = NT // HB

    FC = 7
    GE = FC * P
    SLOTS = 4
    NG = -(-E // (GE * SLOTS)) * SLOTS
    TURNS = NG // SLOTS
    GPP = 2
    EP = NG // GPP
    EW = GPP * GE
    EFULL = E // EW
    FAR = -1

    GC = 125
    GN = E // GC
    GV = 17
    ZB = 2 * GC
    NZ = N // ZB + 1
    assert N == NPART * NT == GC * NT and E == GC * GN and N % ZB == 0 and NT % QB == 0 and NT % HB == 0

    q_dram = nc.dram_tensor("q_table", (ROWS, 3 * D1), BF16).ap()
    rel_dram = nc.dram_tensor("relation_table", (R, 3 * CK), BF16).ap()
    z_dram = nc.dram_tensor("z_rows", (ROWS, UW), F32).ap()
    meta_dram = nc.dram_tensor("edge_meta", (NG, P, FC * 3), I32).ap()
    drel_dram = nc.dram_tensor("edge_window_row", (NG, GE), BF16).ap()
    typ_dram = nc.dram_tensor("edge_relation", (NG, GE), BF16).ap()

    with ExitStack() as ctx:
        def sb(name, shape, dt):
            return ctx.enter_context(nc.sbuf_tensor(name, shape, dt))

        def psum(name, shape, dt):
            return ctx.enter_context(nc.psum_tensor(name, shape, dt))

        def sem(name):
            return ctx.enter_context(nc.semaphore(name))

        ident = sb("ident", [P, P], F32)
        iota_pi = sb("iota_pi", [P, 1], I32)
        iota_ri = sb("iota_ri", [P, P], I32)
        iota_p = sb("iota_p", [P, 1], F32)
        iota_r = sb("iota_r", [P, P], F32)
        upper = sb("upper", [P, P], F32)
        spare_row = sb("spare_row", [P, 1], F32)
        ones = sb("ones", [P, 1], F32)
        zero = sb("zero", [P, 2 * UW], F32)
        xr = sb("xr", [NPART, NT * D], F32)
        a1 = sb("a1", [D, D1], F32)
        a2 = sb("a2", [D, D1], F32)
        rel = sb("rel", [R, D], F32)
        relT = sb("relT", [D, R], F32)
        bmat = sb("bmat", [D1, D1], F32)
        wf = sb("wf", [P, KB, D], F32)
        ws = sb("ws", [D, D], F32)
        xT = sb("xT", [D1, 2, QB * NPART], F32)
        relf = sb("relf", [R, CK], F32)
        relr = sb("relr", [R, CK], F32)
        rel3 = sb("rel3", [R, 3, CK], BF16)
        qf = sb("qf", [NPART, NT * D1], F32)
        qr = sb("qr", [NPART, NT * D1], F32)
        q3 = sb("q3", [NPART, NT, 3, D1], BF16)
        flag = sb("flag", [1, 1], I32)
        bases = sb("bases", [1, NG], I32)

        f_meta = sb("f_meta", [P, SLOTS, FC, 3], I32)
        f_drel = sb("f_drel", [P, SLOTS, GE], BF16)
        f_typ = sb("f_typ", [R, SLOTS, GE], BF16)
        f_q = sb("f_q", [P, SLOTS, 3, D1], BF16)
        f_x = sb("f_x", [P, SLOTS, FC, D1], F32)
        f_dT = sb("f_dT", [P, 2, GE], BF16)
        f_rT = sb("f_rT", [R, 2, GE], BF16)
        f_s = sb("f_s", [P, 2, FC, P], F32)
        f_u = sb("f_u", [P, 2 * FC * UW], F32)
        f_prod = sb("f_prod", [P, FC, D1], F32)
        f_sc = sb("f_sc", [P, 2, FC], F32)
        f_th = sb("f_th", [P, 2, FC], F32)
        f_w = sb("f_w", [P, 2, FC, NB + 1], F32)
        f_zs = sb("f_zs", [P, UW], F32)
        f_zts = sb("f_zts", [P, KB + 1, P], F32)
        acc = sb("acc", [P, ROWS], F32)
        accT = acc[HP:HP + D, :]
        fu = f_u[:].rearrange("p (s c b d) -> p s c b d", s=2, c=FC, b=NB + 1)
        fu2 = f_u[:].rearrange("p (s c w) -> p s c w", s=2, c=FC)

        e_dst, e_next, e_src, e_typ = (f_u[0:EP, k * EW:(k + 1) * EW].bitcast(I32) for k in range(4))
        e_meta = acc[0:EP, 0:3 * EW].bitcast(I32).rearrange("p (e c) -> p e c", c=3)
        e_metaf = acc[0:EP, 0:3 * EW].rearrange("p (e c) -> p e c", c=3)
        e_drel16 = acc[0:EP, 3 * EW:3 * EW + EW // 2].bitcast(BF16)
        e_typ16 = acc[0:EP, 3 * EW + EW // 2:4 * EW].bitcast(BF16)
        e_bad = acc[0:EP, 4 * EW:5 * EW]
        e_badn = sb("e_badn", [EP, 1], F32)

        g_idx = sb("g_idx", [GC, 3], I32)
        g_sidx = sb("g_sidx", [GC, 1], I32)
        g_row = sb("g_row", [GC, GC], I32)
        g_x = sb("g_x", [GC, D1], F32)
        g_q = sb("g_q", [GC, 3 * D1], BF16)
        g_rel = sb("g_rel", [GC, 3 * CK], BF16)
        g_v = sb("g_v", [GC, D1], F32)
        g_c = sb("g_c", [GC, CK], F32)
        g_sc = sb("g_sc", [GC, 4], F32)
        g_w = sb("g_w", [GC, NB + 1], F32)
        g_same = f_s[0:GC, 0, 0, 0:GC]
        g_later = f_s[0:GC, 0, 1, 0:GC]
        g_z = f_u[0:GC, 0:UW]
        g_u = f_u[0:GC, UW:2 * UW]
        g_new = f_u[0:GC, 2 * UW:3 * UW]
        g_zrow = f_u[0:GC, 3 * UW:4 * UW]

        y = qf[:, 0:NT * D].rearrange("p (t d) -> p t d", d=D)
        y2 = qr[:, 0:NT * D].rearrange("p (t d) -> p t d", d=D)
        mean = sb("mean", [NPART, NT], F32)
        var = sb("var", [NPART, NT], F32)

        ps = [psum(f"ps{i}", [P, 512], F32) for i in range(8)]
        z_ps = [ps[0:2], ps[2:4]]
        vq_ps = [ps[4][:, 0:FC * CK].rearrange("p (c k) -> p c k", c=FC), ps[5][:, 0:FC * CK].rearrange("p (c k) -> p c k", c=FC)]
        zt_ps, zl_ps, h_ps = ps[6], ps[7][0:D, 0:P], ps[7][HP:HP + D, 0:P]

        e_set = sem("e_set")
        e_loaded = sem("e_loaded")
        e_made = sem("e_made")
        e_cast = sem("e_cast")
        e_count = sem("e_count")
        e_stored = sem("e_stored")
        bases_loaded = sem("bases_loaded")
        flag_set = sem("flag_set")
        w_loaded = sem("w_loaded")
        x_loaded = sem("x_loaded")
        pool_const = sem("pool_const")
        const = sem("const")
        small_mm = sem("small_mm")
        small_copied = sem("small_copied")
        xT_turned = sem("xT_turned")
        xT_copied = sem("xT_copied")
        q_made = sem("q_made")
        q_copied = sem("q_copied")
        split = sem("split")
        tables = sem("tables")
        acc_clear = sem("acc_clear")
        loaded = [sem(f"loaded{k}") for k in range(SLOTS)]
        gathered = [sem(f"gathered{k}") for k in range(SLOTS)]
        sp_turn = sem("sp_turn")
        pool_turn = sem("pool_turn")
        onehots = sem("onehots")
        vq_ready = sem("vq_ready")
        prod_ready = sem("prod_ready")
        s_ready = sem("s_ready")
        score_ready = sem("score_ready")
        tanh_ready = sem("tanh_ready")
        last_ready = sem("last_ready")
        w_ready = sem("w_ready")
        u_ready = sem("u_ready")
        scattered = sem("scattered")
        z_copied = sem("z_copied")
        zt_turned = sem("zt_turned")
        zt_copied = sem("zt_copied")
        h_summed = sem("h_summed")
        h_added = sem("h_added")
        g_loaded = [sem(f"g_loaded{k}") for k in range(4)]
        g_gathered = [sem(f"g_gathered{k}") for k in range(4)]
        g_cleared = sem("g_cleared")
        g_vec = sem("g_vec")
        g_tanh = sem("g_tanh")
        g_summed = sem("g_summed")
        g_scattered = sem("g_scattered")
        r_loaded = sem("r_loaded")
        r_turned = sem("r_turned")
        r_copied = sem("r_copied")
        r_summed = sem("r_summed")
        r_stored = sem("r_stored")
        h_done = sem("h_done")
        h_turned = sem("h_turned")
        y_ready = sem("y_ready")
        norm = sem("norm")
        std_ready = sem("std_ready")
        out_stored = sem("out_stored")

        block = ctx.enter_context(nc.Block())

        def col(ap):
            return ap.rearrange("(a b) -> a b", b=1)

        @block.sync
        def _(sp):
            sp.wait_ge(e_set, 4)
            for tile, array, skip in ((e_dst, dst, 0), (e_next, dst, 1), (e_src, src, 0), (e_typ, etype, 0)):
                sp.dma_start(tile[0:EFULL, :], array[skip:skip + EFULL * EW].rearrange("(p c) -> p c", c=EW)).then_inc(e_loaded, 16)
                sp.dma_start(tile[EFULL:EFULL + 1, 0:E - EFULL * EW - skip],
                             array[skip + EFULL * EW:E].rearrange("(p c) -> p c", p=1)).then_inc(e_loaded, 16)
            sp.dma_start(a1[:, 0:D], a1_w).then_inc(w_loaded, 16)
            sp.dma_start(a1[:, D:D1], col(a1_b)).then_inc(w_loaded, 16)
            sp.dma_start(a2[:, 0:D], a2_w).then_inc(w_loaded, 16)
            sp.dma_start(a2[:, D:D1], col(a2_b)).then_inc(w_loaded, 16)
            sp.dma_start(rel[:], rel_emb).then_inc(w_loaded, 16)
            sp.dma_start(relf[:, 0:NB], w_comp).then_inc(w_loaded, 16)
            sp.dma_start(wf[:], weight.rearrange("(k b) i o -> (b i) k o", k=KB)).then_inc(w_loaded, 16)
            sp.dma_start(ws[:], w_self).then_inc(w_loaded, 16)
            sp.dma_start(xr[:], x.rearrange("(p t) d -> p (t d)", t=NT)).then_inc(x_loaded, 16)
            sp.dma_start(bases[:], dst[0:E:GE].rearrange("(p c) -> p c", p=1),
                         allow_slow_non_contiguous=True).then_inc(bases_loaded, 16)
            sp.wait_ge(e_made, 2)
            sp.wait_ge(e_cast, 3)
            sp.dma_start(meta_dram.rearrange("(p a) q c -> p (a q c)", a=GPP), e_meta.rearrange("p e c -> p (e c)")).then_inc(e_stored, 16)
            sp.dma_start(drel_dram.rearrange("(p a) e -> p (a e)", a=GPP), e_drel16).then_inc(e_stored, 16)
            sp.dma_start(typ_dram.rearrange("(p a) e -> p (a e)", a=GPP), e_typ16).then_inc(e_stored, 16)
            sp.wait_ge(pool_const, 1)
            sp.dma_start(q_dram[N:ROWS, :], zero[:].bitcast(BF16)[:, 0:3 * D1]).then_inc(tables, 16)
            sp.wait_ge(split, 10)
            sp.dma_start(q_dram[0:N, :].rearrange("(p t) c -> p (t c)", t=NT), q3[:].rearrange("p t a c -> p (t a c)")).then_inc(tables, 16)
            sp.dma_start(rel_dram, rel3[:].rearrange("r a c -> r (a c)")).then_inc(tables, 16)
            sp.wait_ge(tables, 48)
            sp.wait_ge(e_stored, 48)
            sp.wait_ge(bases_loaded, 16)
            sp.wait_ge(flag_set, 1)
            general = sp.value_load(flag[0:1, 0:1], min_val=0, max_val=2 * E)

            def load(g, k):
                base = sp.value_load(bases[0:1, bass.ds(g, 1)], min_val=0, max_val=N - 1)
                sp.dma_start(f_q[:, k].rearrange("p a c -> p (a c)"), q_dram[bass.ds(base, P), :]).then_inc(loaded[k], 16)
                sp.dma_start(f_meta[:, k].rearrange("p c m -> p (c m)"), meta_dram[bass.ds(g, 1)].rearrange("a p m -> (a p) m")).then_inc(loaded[k], 16)
                sp.dma_start(f_drel[:, k, :], drel_dram[bass.ds(g, 1), :].broadcast_to([P, GE])).then_inc(loaded[k], 16)
                sp.dma_start(f_typ[:, k, :], typ_dram[bass.ds(g, 1), :].broadcast_to([R, GE])).then_inc(loaded[k], 16)

            with sp.If(general > 0):
                sp.dma_start(z_dram[0:P, :], zero[:, 0:UW]).then_inc(g_cleared, 16)
                for k in range(NZ - 1):
                    sp.dma_start(z_dram[P + k * ZB:P + (k + 1) * ZB, :].rearrange("(p r) c -> p (r c)", r=2), zero[0:GC, :]).then_inc(g_cleared, 16)
                sp.wait_ge(g_cleared, NZ * 16)
                with sp.Fori(0, GN) as i:
                    sp.dma_start(g_idx[:, 0:1], col(src[bass.ds(i * GC, GC)])).then_inc(g_loaded[0], 16)
                    sp.dma_start(g_idx[:, 1:2], col(dst[bass.ds(i * GC, GC)])).then_inc(g_loaded[1], 16)
                    sp.dma_start(g_idx[:, 2:3], col(etype[bass.ds(i * GC, GC)])).then_inc(g_loaded[2], 16)
                    sp.dma_start(g_row[:], dst[bass.ds(i * GC, GC)].rearrange("(a b) -> a b", a=1).broadcast_to([GC, GC])).then_inc(g_loaded[3], 16)
                    sp.wait_ge(g_scattered, i * 16 + 16).then_inc(sp_turn, 1)
                sp.dma_start(g_zrow, z_dram[0:GC, :]).then_inc(r_loaded, 16)
                with sp.Fori(1, NT) as t:
                    sp.wait_ge(r_turned, t).then_inc(sp_turn, 1)
                    sp.dma_start(g_zrow, z_dram[bass.ds(t * GC, GC), :]).then_inc(r_loaded, 16)
            with sp.Else():
                for k in range(SLOTS):
                    load(k, k)
                with sp.Fori(1, TURNS) as i:
                    for k in range(SLOTS):
                        sp.wait_ge(u_ready, i * (SLOTS * FC) + (k + 1 - SLOTS) * FC).then_inc(sp_turn, 1)
                        load(i * SLOTS + k, k)
            sp.wait_ge(norm, 7)
            sp.dma_start(out.rearrange("(p t) d -> p (t d)", t=NT), y2.rearrange("p t d -> p (t d)")).then_inc(out_stored, 16)
            sp.wait_ge(out_stored, 16)

        @block.gpsimd
        def _(pool):
            for tile, value in ((e_dst, FAR), (e_next, FAR), (e_src, 0), (e_typ, 0)):
                nc.gpsimd.memset(tile, value).then_inc(e_set, 1)
            nc.gpsimd.memset(zero[:], 0.0).then_inc(pool_const, 1)
            nc.gpsimd.memset(ident[:], 0.0).then_inc(pool_const, 1)
            nc.gpsimd.iota(iota_pi[:], pattern=[[0, 1]], base=0, channel_multiplier=1).then_inc(pool_const, 1)
            nc.gpsimd.iota(iota_ri[:], pattern=[[1, P]], base=0, channel_multiplier=0).then_inc(pool_const, 1)
            pool.wait_ge(pool_const, 2)
            nc.gpsimd.affine_select(out=ident[:], in_=ident[:], compare_op=ALU.not_equal, fill=1.0, base=0,
                                    pattern=[[-1, P]], channel_multiplier=1).then_inc(pool_const, 1)
            pool.wait_ge(tables, 48)
            pool.wait_ge(flag_set, 1)
            general = pool.value_load(flag[0:1, 0:1], min_val=0, max_val=2 * E)

            def gather(into, table, index):
                return nc.gpsimd.indirect_dma_start(into, None, table, bass.IndirectOffsetOnAxis(ap=index, axis=0))

            with pool.If(general > 0):
                pool.wait_ge(g_cleared, NZ * 16)
                with pool.Fori(0, GN) as i:
                    for k in range(4):
                        pool.wait_ge(g_loaded[k], i * 16 + 16).then_inc(pool_turn, 1)
                    gather(g_x[:, 0:D], x, g_idx[:, 0:1]).then_inc(g_gathered[0], 16)
                    gather(g_q[:], q_dram, g_idx[:, 1:2]).then_inc(g_gathered[1], 16)
                    gather(g_rel[:], rel_dram, g_idx[:, 2:3]).then_inc(g_gathered[2], 16)
                    gather(g_z, z_dram, g_idx[:, 1:2]).then_inc(g_gathered[3], 16)
                    pool.wait_ge(g_vec, i * GV + GV).then_inc(pool_turn, 1)
                    nc.gpsimd.indirect_dma_start(z_dram, bass.IndirectOffsetOnAxis(ap=g_sidx[:], axis=0), g_new, None).then_inc(g_scattered, 16)
            with pool.Else():
                with pool.Fori(0, TURNS) as i:
                    for k in range(SLOTS):
                        pool.wait_ge(loaded[k], i * 64 + 64).then_inc(pool_turn, 1)
                        for c in range(FC):
                            gather(f_x[:, k, c, 0:D], x, f_meta[:, k, c, 0:1]).then_inc(gathered[k], 16)

        @block.scalar
        def _(act):
            act.wait_ge(e_loaded, 128)
            nc.scalar.copy(e_meta[:, :, 0], e_src).then_inc(e_cast, 1)
            nc.scalar.copy(e_typ16, e_typ).then_inc(e_cast, 1)
            act.wait_ge(e_made, 1)
            nc.scalar.copy(e_drel16, e_metaf[:, :, 1]).then_inc(e_cast, 1)
            for b in range(NQ):
                act.wait_ge(xT_turned, b + 1)
                if b >= 2:
                    act.wait_ge(q_made, b - 1)
                nc.scalar.copy(xT[0:D, b % 2, :], ps[b % 2][0:D, 0:QB * NPART]).then_inc(xT_copied, 1)
            act.wait_ge(flag_set, 1)
            general = act.value_load(flag[0:1, 0:1], min_val=0, max_val=2 * E)

            def tanh(g, k):
                if k >= 0:
                    act.wait_ge(score_ready, g + 1)
                nc.scalar.activation(f_th[:, k % 2, :], f_sc[:, k % 2, :], ACT.Tanh, scale=SCALE).then_inc(tanh_ready, 1)

            def last_flags(g, k, first):
                if not first:
                    act.wait_ge(u_ready, (g - 1) * FC)
                act.wait_ge(gathered[k], turn_of(g, k) * 16 * FC + 16 * FC)
                nc.scalar.copy(f_w[:, k % 2, :, NB], f_meta[:, k].bitcast(F32)[:, :, 2]).then_inc(last_ready, 1)

            def copy_z(g, k, first):
                act.wait_ge(scattered, g + 1)
                if not first:
                    act.wait_ge(zt_turned, g)
                for h in range(2):
                    nc.scalar.copy(f_zs[:, h * HALF:(h + 1) * HALF], z_ps[k % 2][h][:, 0:HALF]).then_inc(z_copied, 1)

            def copy_zt(g, first):
                act.wait_ge(zt_turned, g + 1)
                if not first:
                    act.wait_ge(h_summed, g)
                nc.scalar.copy(f_zts[:, 0:KB, :].rearrange("p k n -> p (k n)"), zt_ps[:]).then_inc(zt_copied, 1)
                nc.scalar.copy(f_zts[0:D, KB, :], zl_ps).then_inc(zt_copied, 1)

            def turn_of(g, k):
                return (g - k) // SLOTS if isinstance(g, int) else turn_reg[0]

            turn_reg = [None]

            with act.If(general > 0):
                with act.Fori(0, GN) as i:
                    act.wait_ge(g_vec, i * GV + 8)
                    nc.scalar.activation(g_sc[:, 1:2], g_sc[:, 0:1], ACT.Tanh, scale=SCALE).then_inc(g_tanh, 1)
                with act.Fori(0, NT) as t:
                    act.wait_ge(r_turned, t + 1)
                    nc.scalar.copy(f_zts[:, 0:KB, 0:GC], ps[0][:, 0:KB * GC].rearrange("p (k n) -> p k n", k=KB)).then_inc(r_copied, 1)
                    nc.scalar.copy(f_zts[0:D, KB, 0:GC], ps[1][0:D, 0:GC]).then_inc(r_copied, 1)
                act.nop()
            with act.Else():
                def turn(i, peel):
                    turn_reg[0] = i
                    for k in range(SLOTS):
                        g = i * SLOTS + k
                        last_flags(g, k, peel and k < 2)
                        tanh(g, k)
                        if not (peel and k == 0):
                            copy_z(g - 1, k - 1, peel and k == 1)
                            copy_zt(g - 1, peel and k == 1)
                turn(0, True)
                with act.Fori(1, TURNS) as i:
                    turn(i, False)
                copy_z(NG - 1, NG - 1, False)
                copy_zt(NG - 1, False)
            act.wait_ge(norm, 5)
            nc.scalar.activation(mean[:], var[:], ACT.Sqrt).then_inc(std_ready, 1)

        @block.tensor
        def _(pe):
            pe.wait_ge(pool_const, 5)
            pe.wait_ge(w_loaded, 128)
            nc.tensor.transpose(ps[4][0:D, 0:R], rel[:], ident[0:R, 0:R]).then_inc(small_mm, 1)
            nc.tensor.matmul(ps[5][0:D1, 0:D1], a2[:], a1[:], start=True, stop=True).then_inc(small_mm, 1)
            pe.wait_ge(small_copied, 1)
            nc.tensor.matmul(ps[6][0:R, 0:D1], relT[:], a1[:], start=True, stop=True).then_inc(small_mm, 1)
            pe.wait_ge(e_count, 1)
            pe.wait_ge(const, 7)
            nc.tensor.matmul(ps[7][0:1, 0:1], e_badn[:], ones[0:EP, :], start=True, stop=True).then_inc(small_mm, 1)
            pe.wait_ge(x_loaded, 16)
            pe.wait_ge(small_copied, 3)

            def make_q(b):
                pe.wait_ge(xT_copied, b + 1)
                if b >= 2:
                    pe.wait_ge(q_copied, b - 1)
                for j in range(QB):
                    last = nc.tensor.matmul(ps[2 + b % 2][0:NPART, j * D1:(j + 1) * D1], xT[:, b % 2, j * NPART:(j + 1) * NPART],
                                            bmat[:], start=True, stop=True)
                last.then_inc(q_made, 1)

            for b in range(NQ):
                if b >= 2:
                    pe.wait_ge(xT_copied, b - 1)
                for j in range(QB):
                    t = b * QB + j
                    last = nc.tensor.transpose(ps[b % 2][0:D, j * NPART:(j + 1) * NPART], xr[:, t * D:(t + 1) * D], ident[0:NPART, 0:NPART])
                last.then_inc(xT_turned, 1)
                if b >= 1:
                    make_q(b - 1)
            make_q(NQ - 1)
            pe.wait_ge(flag_set, 1)
            general = pe.value_load(flag[0:1, 0:1], min_val=0, max_val=2 * E)

            def add_vq(g, k):
                pe.wait_ge(onehots, g + 1)
                for c in range(FC):
                    out_c = vq_ps[k % 2][:, c, :]
                    for a in range(3):
                        nc.tensor.matmul(out_c, f_rT[:, k % 2, c:GE:FC], rel3[:, a, :], start=(a == 0), stop=False)
                    for a in range(3):
                        last = nc.tensor.matmul(out_c[:, NB:CK], f_dT[:, k % 2, c:GE:FC], f_q[:, k, a, :], start=False, stop=(a == 2))
                last.then_inc(vq_ready, 1)

            def scatter(g, k, chunks, first):
                if chunks[0] == 0 and not first:
                    pe.wait_ge(z_copied, (g - 1) * 2)
                for c in chunks:
                    pe.wait_ge(u_ready, g * FC + c + 1)
                    for h in range(2):
                        last = nc.tensor.matmul(z_ps[k % 2][h][:, 0:HALF], f_s[:, k % 2, c, :], fu2[:, k % 2, c, h * HALF:(h + 1) * HALF],
                                                start=(c == 0), stop=(c == FC - 1))
                if chunks[-1] == FC - 1:
                    last.then_inc(scattered, 1)

            def turn_z(g, first):
                pe.wait_ge(z_copied, g * 2 + 2)
                if not first:
                    pe.wait_ge(zt_copied, g * 2)
                for b in range(KB):
                    nc.tensor.transpose(zt_ps[:, b * P:(b + 1) * P], f_zs[:, b * P:(b + 1) * P], ident[:])
                nc.tensor.transpose(zl_ps, f_zs[:, KB * P:UW], ident[:]).then_inc(zt_turned, 1)

            def weigh(g, first):
                pe.wait_ge(zt_copied, g * 2 + 2)
                if not first:
                    pe.wait_ge(h_added, g)
                for b in range(KB):
                    nc.tensor.matmul(h_ps, wf[:, b, :], f_zts[:, b, :], start=(b == 0), stop=False)
                nc.tensor.matmul(h_ps, ws[:], f_zts[0:D, KB, :], start=False, stop=True).then_inc(h_summed, 1)

            with pe.If(general > 0):
                with pe.Fori(0, GN) as i:
                    pe.wait_ge(g_vec, i * GV + 15)
                    for h in range(2):
                        last = nc.tensor.matmul(ps[h][0:GC, 0:HALF], g_same, g_u[:, h * HALF:(h + 1) * HALF], start=True, stop=True)
                    last.then_inc(g_summed, 1)
                with pe.Fori(0, NT) as t:
                    pe.wait_ge(r_loaded, t * 16 + 16)
                    for b in range(KB):
                        nc.tensor.transpose(ps[0][:, b * GC:(b + 1) * GC], g_zrow[:, b * P:(b + 1) * P], ident[0:GC, 0:GC])
                    nc.tensor.transpose(ps[1][0:D, 0:GC], g_zrow[:, KB * P:UW], ident[0:GC, 0:GC]).then_inc(r_turned, 1)
                    pe.wait_ge(r_copied, t * 2 + 2)
                    for b in range(KB):
                        nc.tensor.matmul(ps[2][HP:HP + D, 0:GC], wf[:, b, :], f_zts[:, b, 0:GC], start=(b == 0), stop=False)
                    nc.tensor.matmul(ps[2][HP:HP + D, 0:GC], ws[:], f_zts[0:D, KB, 0:GC], start=False, stop=True).then_inc(r_summed, 1)
                    pe.wait_ge(r_stored, t + 1)
                pe.nop()
            with pe.Else():
                def turn(i, peel, end):
                    for k in range(SLOTS):
                        g = i * SLOTS + k
                        if not (end and k == SLOTS - 1):
                            add_vq(g + 1, (k + 1) % SLOTS)
                        if not (peel and k == 0):
                            turn_z(g - 1, peel and k == 1)
                        scatter(g, k, (0, 1, 2, 3), peel and k < 2)
                        if not (peel and k == 0):
                            weigh(g - 1, peel and k == 1)
                        scatter(g, k, (4, 5, 6), False)
                add_vq(0, 0)
                turn(0, True, False)
                with pe.Fori(1, TURNS - 1) as i:
                    turn(i, False, False)
                turn(TURNS - 1, False, True)
                turn_z(NG - 1, False)
                weigh(NG - 1, False)
            pe.wait_ge(h_done, 1)
            for b in range(NH):
                if b >= 4:
                    pe.wait_ge(y_ready, b - 3)
                for j in range(HB):
                    t = b * HB + j
                    last = nc.tensor.transpose(ps[b % 4][0:NPART, j * D:(j + 1) * D], accT[:, t:N:NT], ident[HP:HP + D, HP:HP + D])
                last.then_inc(h_turned, 1)

        @block.vector
        def _(dve):
            nc.vector.memset(xT[D:D1, :, :], 1.0).then_inc(const, 1)
            nc.vector.memset(g_x[:, D:D1], 1.0).then_inc(const, 1)
            nc.vector.memset(ones[:], 1.0).then_inc(const, 1)
            nc.vector.memset(f_x[:, :, :, D], 1.0).then_inc(const, 1)
            dve.wait_ge(pool_const, 4)
            nc.vector.tensor_copy(iota_p[:], iota_pi[:]).then_inc(const, 1)
            nc.vector.tensor_copy(iota_r[:], iota_ri[:]).then_inc(const, 1)
            dve.wait_ge(const, 6)
            nc.vector.tensor_scalar(upper[:], iota_r[:], iota_p[:, 0:1], None, ALU.is_gt).then_inc(const, 1)
            nc.vector.tensor_scalar(spare_row[:], iota_p[:], float(N), None, ALU.add).then_inc(const, 1)
            dve.wait_ge(e_loaded, 128)
            grouped = e_dst.rearrange("p (a e) -> p a e", a=GPP)
            nc.vector.tensor_tensor(e_metaf[:, :, 1].rearrange("p (a e) -> p a e", a=GPP), grouped,
                                    grouped[:, :, 0:1].broadcast_to([EP, GPP, GE]), ALU.subtract).then_inc(e_made, 1)
            nc.vector.tensor_tensor(e_metaf[:, :, 2], e_dst, e_next, ALU.not_equal).then_inc(e_made, 1)
            nc.vector.tensor_tensor(e_bad, e_dst, e_next, ALU.is_gt).then_inc(e_made, 1)
            dve.wait_ge(e_made, 3)
            nc.vector.scalar_tensor_tensor(out=e_bad, in0=e_metaf[:, :, 1], scalar=float(P), in1=e_bad,
                                           op0=ALU.is_ge, op1=ALU.add).then_inc(e_made, 1)
            dve.wait_ge(e_made, 4)
            nc.vector.tensor_reduce(e_badn[:], e_bad, AX_X, ALU.add).then_inc(e_count, 1)
            dve.wait_ge(small_mm, 1)
            nc.vector.tensor_copy(relT[:], ps[4][0:D, 0:R]).then_inc(small_copied, 1)
            dve.wait_ge(small_mm, 2)
            nc.vector.tensor_copy(bmat[:], ps[5][0:D1, 0:D1]).then_inc(small_copied, 1)
            dve.wait_ge(small_mm, 3)
            nc.vector.tensor_copy(relf[:, NB:CK], ps[6][0:R, 0:D1]).then_inc(small_copied, 1)
            dve.wait_ge(small_mm, 4)
            nc.vector.tensor_scalar(flag[:], ps[7][0:1, 0:1], -1.0, None, ALU.add).then_inc(flag_set, 1)
            for b in range(NQ):
                dve.wait_ge(q_made, b + 1)
                nc.vector.tensor_copy(qf[:, b * QB * D1:(b + 1) * QB * D1], ps[2 + b % 2][0:NPART, 0:QB * D1]).then_inc(q_copied, 1)
            dve.wait_ge(small_copied, 3)
            dve.wait_ge(q_copied, NQ)
            qf3, qr3 = (t[:].rearrange("p (t c) -> p t c", c=D1) for t in (qf, qr))
            n = 0
            for full, rest, parts in ((relf[:], relr[:], [rel3[:, a, :] for a in range(3)]), (qf3, qr3, [q3[:, :, a, :] for a in range(3)])):
                nc.vector.tensor_copy(parts[0], full).then_inc(split, 1)
                dve.wait_ge(split, n + 1)
                nc.vector.tensor_tensor(rest, full, parts[0], ALU.subtract).then_inc(split, 1)
                dve.wait_ge(split, n + 2)
                nc.vector.tensor_copy(parts[1], rest).then_inc(split, 1)
                dve.wait_ge(split, n + 3)
                nc.vector.tensor_tensor(full, rest, parts[1], ALU.subtract).then_inc(split, 1)
                dve.wait_ge(split, n + 4)
                nc.vector.tensor_copy(parts[2], full).then_inc(split, 1)
                n += 5
            dve.wait_ge(e_stored, 48)
            nc.vector.memset(accT, 0.0).then_inc(acc_clear, 1)
            dve.wait_ge(acc_clear, 1)
            dve.wait_ge(const, 8)
            dve.wait_ge(bases_loaded, 16)
            dve.wait_ge(flag_set, 1)
            general = dve.value_load(flag[0:1, 0:1], min_val=0, max_val=2 * E)

            def one_hots(g, k, turn_no):
                dve.wait_ge(loaded[k], turn_no * 64 + 64)
                nc.vector.tensor_scalar(f_dT[:, k % 2, :], f_drel[:, k, :], iota_p[:, 0:1], None, ALU.is_equal)
                nc.vector.tensor_scalar(f_rT[:, k % 2, :], f_typ[:, k, :], iota_p[0:R, 0:1], None, ALU.is_equal).then_inc(onehots, 1)

            def score(g, k, turn_no, first):
                dve.wait_ge(vq_ready, g + 1)
                dve.wait_ge(gathered[k], turn_no * 16 * FC + 16 * FC)
                nc.vector.tensor_tensor(f_prod[:], vq_ps[k % 2][:, :, NB:CK], f_x[:, k], ALU.mult).then_inc(prod_ready, 1)
                if not first:
                    dve.wait_ge(scattered, g - 1)
                for c in range(FC):
                    last = nc.vector.tensor_scalar(f_s[:, k % 2, c, :], iota_r[:], f_meta[:, k].bitcast(F32)[:, c, 1:2], None, ALU.is_equal)
                dve.wait_ge(prod_ready, g + 1)
                nc.vector.tensor_reduce(f_sc[:, k % 2, :], f_prod[:], AX_X, ALU.add).then_inc(score_ready, 1)

            def spread(g, k):
                dve.wait_ge(tanh_ready, g + 1)
                nc.vector.scalar_tensor_tensor(out=f_w[:, k % 2, :, 0:NB], in0=f_th[:, k % 2, :].rearrange("p (c o) -> p c o", o=1).broadcast_to([P, FC, NB]),
                                               scalar=0.0, in1=vq_ps[k % 2][:, :, 0:NB], op0=ALU.max, op1=ALU.mult).then_inc(w_ready, 1)
                dve.wait_ge(w_ready, g + 1)
                dve.wait_ge(last_ready, g + 1)
                for c in range(FC):
                    nc.vector.tensor_tensor(fu[:, k % 2, c], f_w[:, k % 2, c, :].rearrange("p (b o) -> p b o", o=1).broadcast_to([P, NB + 1, D]),
                                            f_x[:, k, c, 0:D].rearrange("p (o d) -> p o d", o=1).broadcast_to([P, NB + 1, D]),
                                            ALU.mult).then_inc(u_ready, 1)

            def add_h(g, base, first):
                dve.wait_ge(h_summed, g + 1)
                if not first:
                    dve.wait_ge(h_added, g)
                window = accT[:, bass.ds(base, P)]
                nc.vector.tensor_tensor(window, window, h_ps, ALU.add).then_inc(h_added, 1)

            with dve.If(general > 0):
                with dve.Fori(0, GN) as i:
                    for k in range(4):
                        dve.wait_ge(g_gathered[k], i * 16 + 16)
                    nc.vector.tensor_tensor(g_v[:], g_q[:, 0:D1], g_q[:, D1:2 * D1], ALU.add).then_inc(g_vec, 1)
                    dve.wait_ge(g_vec, i * GV + 1)
                    nc.vector.tensor_tensor(g_v[:], g_v[:], g_q[:, 2 * D1:3 * D1], ALU.add).then_inc(g_vec, 1)
                    nc.vector.tensor_tensor(g_c[:], g_rel[:, 0:CK], g_rel[:, CK:2 * CK], ALU.add).then_inc(g_vec, 1)
                    dve.wait_ge(g_vec, i * GV + 3)
                    nc.vector.tensor_tensor(g_c[:], g_c[:], g_rel[:, 2 * CK:3 * CK], ALU.add).then_inc(g_vec, 1)
                    dve.wait_ge(g_vec, i * GV + 4)
                    nc.vector.tensor_tensor(g_v[:], g_v[:], g_c[:, NB:CK], ALU.add).then_inc(g_vec, 1)
                    nc.vector.tensor_copy(g_sc[:, 2:3], g_idx[:, 1:2]).then_inc(g_vec, 1)
                    dve.wait_ge(g_vec, i * GV + 6)
                    nc.vector.tensor_tensor(g_v[:], g_v[:], g_x[:], ALU.mult).then_inc(g_vec, 1)
                    dve.wait_ge(g_vec, i * GV + 7)
                    nc.vector.tensor_reduce(g_sc[:, 0:1], g_v[:], AX_X, ALU.add).then_inc(g_vec, 1)
                    nc.vector.tensor_scalar(g_same, g_row[:], g_sc[:, 2:3], None, ALU.is_equal).then_inc(g_vec, 1)
                    dve.wait_ge(g_vec, i * GV + 9)
                    nc.vector.tensor_tensor(g_later, g_same, upper[0:GC, 0:GC], ALU.mult).then_inc(g_vec, 1)
                    dve.wait_ge(g_vec, i * GV + 10)
                    nc.vector.tensor_reduce(g_sc[:, 3:4], g_later, AX_X, ALU.add).then_inc(g_vec, 1)
                    dve.wait_ge(g_vec, i * GV + 11)
                    nc.vector.tensor_scalar(g_w[:, NB:NB + 1], g_sc[:, 3:4], 0.0, None, ALU.is_equal).then_inc(g_vec, 1)
                    dve.wait_ge(g_tanh, i + 1)
                    nc.vector.scalar_tensor_tensor(out=g_w[:, 0:NB], in0=g_sc[:, 1:2].broadcast_to([GC, NB]), scalar=0.0, in1=g_c[:, 0:NB],
                                                   op0=ALU.max, op1=ALU.mult).then_inc(g_vec, 1)
                    dve.wait_ge(g_vec, i * GV + 13)
                    nc.vector.tensor_scalar(g_sc[:, 2:3], g_sc[:, 2:3], spare_row[0:GC, 0:1], g_w[:, NB:NB + 1], ALU.subtract, ALU.mult).then_inc(g_vec, 1)
                    nc.vector.tensor_tensor(g_u.rearrange("p (b d) -> p b d", d=D),
                                            g_w[:].rearrange("p (b o) -> p b o", o=1).broadcast_to([GC, NB + 1, D]),
                                            g_x[:, 0:D].rearrange("p (o d) -> p o d", o=1).broadcast_to([GC, NB + 1, D]), ALU.mult).then_inc(g_vec, 1)
                    dve.wait_ge(g_vec, i * GV + 15)
                    nc.vector.tensor_scalar(g_sidx[:], g_sc[:, 2:3], spare_row[0:GC, 0:1], None, ALU.add).then_inc(g_vec, 1)
                    dve.wait_ge(g_summed, i + 1)
                    nc.vector.tensor_tensor(g_new[:, 0:HALF], ps[0][0:GC, 0:HALF], g_z[:, 0:HALF], ALU.add)
                    nc.vector.tensor_tensor(g_new[:, HALF:NB * D], ps[1][0:GC, 0:NB * D - HALF], g_z[:, HALF:NB * D], ALU.add)
                    nc.vector.tensor_copy(g_new[:, NB * D:UW], ps[1][0:GC, NB * D - HALF:HALF]).then_inc(g_vec, 1)
                with dve.Fori(0, NT) as t:
                    dve.wait_ge(r_summed, t + 1)
                    nc.vector.tensor_copy(accT[:, bass.ds(t * GC, GC)], ps[2][HP:HP + D, 0:GC]).then_inc(r_stored, 1)
                dve.wait_ge(r_stored, NT)
                nc.vector.tensor_copy(accT[:, 0:1], accT[:, 0:1]).then_inc(h_done, 1)
            with dve.Else():
                def turn(i, peel, end):
                    for k in range(SLOTS):
                        g = i * SLOTS + k
                        if not (peel and k == 0):
                            base = dve.value_load(bases[0:1, bass.ds(g - 1, 1)], min_val=0, max_val=N - 1)
                        score(g, k, i, peel and k < 2)
                        if not (end and k == SLOTS - 1):
                            one_hots(g + 1, (k + 1) % SLOTS, i if k < SLOTS - 1 else i + 1)
                        spread(g, k)
                        if not (peel and k == 0):
                            add_h(g - 1, base, peel and k == 1)
                one_hots(0, 0, 0)
                turn(0, True, False)
                with dve.Fori(1, TURNS - 1) as i:
                    turn(i, False, False)
                turn(TURNS - 1, False, True)
                base = dve.value_load(bases[0:1, NG - 1:NG], min_val=0, max_val=N - 1)
                add_h(NG - 1, base, False)
                dve.wait_ge(h_added, NG)
                nc.vector.tensor_copy(accT[:, 0:1], accT[:, 0:1]).then_inc(h_done, 1)
            for b in range(NH):
                dve.wait_ge(h_turned, b + 1)
                nc.vector.scalar_tensor_tensor(out=qf[:, b * HB * D:(b + 1) * HB * D], in0=ps[b % 4][0:NPART, 0:HB * D],
                                               scalar=0.0, in1=xr[:, b * HB * D:(b + 1) * HB * D], op0=ALU.max, op1=ALU.add).then_inc(y_ready, 1)
            wide = [NPART, NT, D]

            def rows(ap):
                return ap[:].rearrange("p (t o) -> p t o", o=1).broadcast_to(wide)

            dve.wait_ge(y_ready, NH)
            nc.vector.tensor_reduce(mean[:], y, AX_X, ALU.add).then_inc(norm, 1)
            dve.wait_ge(norm, 1)
            nc.vector.scalar_tensor_tensor(out=y, in0=rows(mean), scalar=-1.0 / D, in1=y, op0=ALU.mult, op1=ALU.add).then_inc(norm, 1)
            dve.wait_ge(norm, 2)
            nc.vector.tensor_tensor(y2, y, y, ALU.mult).then_inc(norm, 1)
            dve.wait_ge(norm, 3)
            nc.vector.tensor_reduce(var[:], y2, AX_X, ALU.add).then_inc(norm, 1)
            dve.wait_ge(norm, 4)
            nc.vector.tensor_scalar(var[:], var[:], 1.0 / D, EPS, ALU.mult, ALU.add).then_inc(norm, 1)
            dve.wait_ge(std_ready, 1)
            nc.vector.reciprocal(var[:], mean[:]).then_inc(norm, 1)
            dve.wait_ge(norm, 6)
            nc.vector.tensor_tensor(y2, y, rows(var), ALU.mult).then_inc(norm, 1)


_INS = ["x", "src", "dst", "edge_type_86", "L0_gnn_weight", "L0_gnn_w_comp", "L0_gnn_self_loop_weight",
        "L0_gnn_A1_w", "L0_gnn_A1_b", "L0_gnn_A2_w", "L0_gnn_A2_b", "L0_gnn_rel_emb"]


def kernel(**inputs):
    import numpy as _np
    import concourse.bacc as _bacc
    from concourse import mybir as _mybir
    from concourse.bass_utils import run_bass_kernel_spmd as _run

    nc = _bacc.Bacc("TRN2", target_bir_lowering=False, num_devices=1)
    arrays, args = {}, []
    for name in _INS:
        a = _np.ascontiguousarray(inputs[name])
        arrays[f"in_{name}"] = a
        args.append(nc.dram_tensor(f"in_{name}", a.shape, _mybir.dt.from_np(a.dtype), kind="ExternalInput").ap())
    out = nc.dram_tensor("out", args[0].shape, F32, kind="ExternalOutput").ap()
    build(nc, *args, out)
    r = _run(nc, [arrays], core_ids=[0])
    return r.results[0]["out"]
```

```python
from contextlib import ExitStack

import concourse.bass as bass
from concourse import mybir

F32 = mybir.dt.float32
BF16 = mybir.dt.bfloat16
I32 = mybir.dt.int32
ALU = mybir.AluOpType
ACT = mybir.ActivationFunctionType
AX_X = mybir.AxisListType.X


def build(nc, x, src, dst, etype, weight, w_comp, w_self, a1_w, a1_b, a2_w, a2_b, rel_emb, out):
    P = 128
    N, D = x.shape
    E = src.shape[0]
    R, NB = w_comp.shape
    D1 = D + 1
    CK = NB + D1
    UW = (NB + 1) * D
    HALF = UW // 2
    KB = NB * D // P
    ROWS = N + P
    SCALE = float(D) ** -0.5
    EPS = 1e-5
    HP = 32

    NPART = 125
    NT = N // NPART
    QB = 4
    QW = QB * D1
    NBLK = NT // QB
    XSPLIT = NBLK // 2 + 1
    BB = 3
    NQ = -(-NBLK // BB)
    PARTS_OF = 3
    QBUF = 4
    QBANK = 3
    CLEAR = 5600
    HB = 5
    NH = NT // HB
    NPIECE = 5
    PT = NT // NPIECE
    DVE_DIVIDES = range(2, NPIECE)

    FC = 6
    HC = FC // 2
    HE = HC * P
    GE = FC * P
    WIN = P // 2
    SLOTS = 10
    RS = 5
    GPP = 3
    NG = -(-E // (GE * GPP)) * GPP
    TURNS = NG // SLOTS - 1
    ENDG = NG - TURNS * SLOTS
    EP = NG // GPP
    EW = GPP * GE
    EFULL = E // EW
    EREST = E - EFULL * EW
    EQ = 64
    NHALF = -(-E // HE)
    FAR = -1
    NOREL = R

    GC = 125
    GN = E // GC
    GV = 17
    ZB = 2 * GC
    NZ = N // ZB + 1
    assert SLOTS == 2 * RS and NHALF == 2 * NG - 1 and N == NPART * NT == GC * NT and E == GC * GN and N % ZB == 0 and NT % QB == 0 and NT % HB == 0
    assert EP <= P and EFULL == EP - 1 and EQ <= EFULL and NT % 2 == 0

    q_dram = nc.dram_tensor("q_table", (ROWS, 3 * D1), BF16).ap()
    rel_dram = nc.dram_tensor("relation_table", (R, 3 * CK), BF16).ap()
    z_dram = nc.dram_tensor("z_rows", (ROWS, UW), F32).ap()
    meta_dram = nc.dram_tensor("edge_meta", (NG, 2, P, HC * 2), I32).ap()
    row_dram = nc.dram_tensor("edge_window_row", (NG, GE), BF16).ap()
    typ_dram = nc.dram_tensor("edge_relation", (NG, GE), BF16).ap()

    with ExitStack() as ctx:
        def sb(name, shape, dt):
            return ctx.enter_context(nc.sbuf_tensor(name, shape, dt))

        def psum(name, shape, dt):
            return ctx.enter_context(nc.psum_tensor(name, shape, dt))

        def sem(name):
            return ctx.enter_context(nc.semaphore(name))

        ident = sb("ident", [P, P], F32)
        ident16 = sb("ident16", [P, P], BF16)
        iota_pi = sb("iota_pi", [P, 1], I32)
        iota_ri = sb("iota_ri", [P, P], I32)
        iota_p = sb("iota_p", [P, 1], F32)
        iota_r = sb("iota_r", [P, P], F32)
        upper = sb("upper", [P, P], F32)
        spare_row = sb("spare_row", [P, 1], F32)
        ones = sb("ones", [P, 1], F32)
        eps = sb("eps", [P, 1], F32)
        root_early = sb("root_early", [P, 1], F32)
        zero = sb("zero", [P, 2 * UW], F32)
        xr = sb("xr", [NPART, NT * D], F32)
        a1 = sb("a1", [D, D1], F32)
        a2 = sb("a2", [D, D1], F32)
        rel = sb("rel", [R, D], F32)
        relT = sb("relT", [D, R], F32)
        wf = sb("wf", [P, KB, D], F32)
        ws = sb("ws", [D, D], F32)
        bblock = sb("bblock", [P, QW], F32)
        a2_bias = sb("a2_bias", [D, NPART], F32)
        q_bias = sb("q_bias", [NPART, D1], F32)
        xT = sb("xT", [P, QBUF, BB * NPART], F32)
        relf = sb("relf", [R, CK], F32)
        relr = sb("relr", [R, CK], F32)
        rel3 = sb("rel3", [R, 3, CK], BF16)
        qf = sb("qf", [NPART, NT * D1], F32)
        qr = sb("qr", [NPART, NT * D1], F32)
        q3_flat = sb("q3", [NPART, NT * 3 * D1], BF16)
        q3 = q3_flat[:].rearrange("p (t a c) -> p t a c", a=3, c=D1)
        flag = sb("flag", [1, 1], I32)
        bases = sb("bases", [1, 2 * NG], I32)

        f_src = sb("f_src", [P, SLOTS, FC], I32)
        f_meta = sb("f_meta", [P, SLOTS, FC, 2], I32)
        f_row = sb("f_row", [P, RS, GE], BF16)
        f_typ = sb("f_typ", [R, RS, GE], BF16)
        f_q = sb("f_q", [P, RS, 3, D1], BF16)
        f_x = sb("f_x", [P, SLOTS, FC, D1], F32)
        f_dT = sb("f_dT", [P, 2, GE], BF16)
        f_rT = sb("f_rT", [R, 2, GE], BF16)
        f_s = sb("f_s", [P, 2, FC, WIN], F32)
        f_u = sb("f_u", [P, 2 * FC * UW], F32)
        f_prod = sb("f_prod", [P, FC, D1], F32)
        f_sc = sb("f_sc", [P, 2, FC], F32)
        f_th = sb("f_th", [P, 2, FC], F32)
        f_w = sb("f_w", [P, 2, FC, NB + 1], F32)
        f_zs = sb("f_zs", [P, UW], F32)
        f_zts = sb("f_zts", [P, KB + 1, P], F32)
        acc = sb("acc", [P, ROWS], F32)
        accT = acc[HP:HP + D, :]
        qf3, qr3 = (t[:].rearrange("p (t c) -> p t c", c=D1) for t in (qf, qr))
        fu = f_u[:].rearrange("p (s c b d) -> p s c b d", s=2, c=FC, b=NB + 1)
        fu2 = f_u[:].rearrange("p (s c w) -> p s c w", s=2, c=FC)

        e_dst = f_u[0:EP, 0:EW + 1].bitcast(I32)
        e_src = f_u[0:EP, EW + 1:2 * EW + 1].bitcast(I32)
        e_meta = acc[0:EP, 0:2 * EW].bitcast(I32).rearrange("p (e c) -> p e c", c=2)
        e_metaf = acc[0:EP, 0:2 * EW].rearrange("p (e c) -> p e c", c=2)
        e_typ = acc[0:EP, 2 * EW:3 * EW].bitcast(I32)
        e_row16 = acc[0:EP, 3 * EW:3 * EW + EW // 2].bitcast(BF16)
        e_typ16 = acc[0:EP, 3 * EW + EW // 2:4 * EW].bitcast(BF16)
        e_down = acc[0:EP, 4 * EW:5 * EW]
        e_shift = sb("e_shift", [EP, 2 * GPP], F32)
        e_count = sb("e_count", [EP, 2 * GPP + 1], F32)
        e_total = sb("e_total", [1, 1], F32)
        e_halves = e_dst[:, 0:EW].rearrange("p (a e) -> p a e", e=HE)

        g_idx = sb("g_idx", [GC, 3], I32)
        g_sidx = sb("g_sidx", [GC, 1], I32)
        g_row = sb("g_row", [GC, GC], I32)
        g_x = sb("g_x", [GC, D1], F32)
        g_q = sb("g_q", [GC, 3 * D1], BF16)
        g_rel = sb("g_rel", [GC, 3 * CK], BF16)
        g_v = sb("g_v", [GC, D1], F32)
        g_c = sb("g_c", [GC, CK], F32)
        g_sc = sb("g_sc", [GC, 4], F32)
        g_w = sb("g_w", [GC, NB + 1], F32)
        g_flat = f_s[:].rearrange("p s c n -> p (s c n)")
        g_same = g_flat[0:GC, 0:GC]
        g_later = g_flat[0:GC, GC:2 * GC]
        g_z = f_u[0:GC, 0:UW]
        g_u = f_u[0:GC, UW:2 * UW]
        g_new = f_u[0:GC, 2 * UW:3 * UW]
        g_zrow = f_u[0:GC, 3 * UW:4 * UW]

        y = qf[:, 0:NT * D].rearrange("p (t d) -> p t d", d=D)
        y2 = qr[:, 0:NT * D].rearrange("p (t d) -> p t d", d=D)
        mean = sb("mean", [NPART, NT], F32)
        var = sb("var", [NPART, NT], F32)

        ps = [psum(f"ps{i}", [P, 512], F32) for i in range(8)]
        z_ps = [ps[0:2], ps[2:4]]
        s_ps = [[bank[:, HALF:HALF + HC * WIN // 2].bitcast(BF16).rearrange("p (c n) -> p c n", c=HC) for bank in z] for z in z_ps]
        vq_ps = [ps[4][:, 0:FC * CK].rearrange("p (c k) -> p c k", c=FC), ps[5][:, 0:FC * CK].rearrange("p (c k) -> p c k", c=FC)]
        zt_ps, zl_ps, h_ps = ps[6], ps[7][0:D, 0:P], ps[7][HP:HP + D, 0:P]

        e_set = sem("e_set")
        first_loaded = [sem(f"first_loaded{n}") for n in range(2)]
        dst_loaded = sem("dst_loaded")
        src_loaded = sem("src_loaded")
        typ_loaded = sem("typ_loaded")
        e_shifted = sem("e_shifted")
        e_row_made = sem("e_row_made")
        e_cast = sem("e_cast")
        last_made = sem("last_made")
        e_checked = sem("e_checked")
        e_stored = sem("e_stored")
        bases_loaded = sem("bases_loaded")
        flag_set = sem("flag_set")
        a_loaded = sem("a_loaded")
        w_loaded = sem("w_loaded")
        x_loaded = [sem(f"x_loaded{n}") for n in range(2)]
        pool_const = sem("pool_const")
        const = sem("const")
        small_mm = sem("small_mm")
        small_copied = sem("small_copied")
        xT_turned = sem("xT_turned")
        xT_copied = sem("xT_copied")
        q_made = sem("q_made")
        q_copied = sem("q_copied")
        split = sem("split")
        q_part = sem("q_part")
        q_rest = sem("q_rest")
        tables = sem("tables")
        acc_clear = sem("acc_clear")
        meta_loaded = [sem(f"meta_loaded{k}") for k in range(SLOTS)]
        rows_loaded = [sem(f"rows_loaded{k}") for k in range(SLOTS)]
        gathered = [sem(f"gathered{k}") for k in range(SLOTS)]
        sp_turn = sem("sp_turn")
        pool_turn = sem("pool_turn")
        onehots = sem("onehots")
        vq_ready = sem("vq_ready")
        prod_ready = sem("prod_ready")
        s_turned = sem("s_turned")
        s_ready = sem("s_ready")
        score_ready = sem("score_ready")
        tanh_ready = sem("tanh_ready")
        last_ready = sem("last_ready")
        w_ready = sem("w_ready")
        u_ready = sem("u_ready")
        scattered = sem("scattered")
        z_copied = sem("z_copied")
        zt_turned = sem("zt_turned")
        zt_copied = sem("zt_copied")
        h_summed = sem("h_summed")
        h_added = sem("h_added")
        g_loaded = [sem(f"g_loaded{k}") for k in range(4)]
        g_gathered = [sem(f"g_gathered{k}") for k in range(4)]
        g_cleared = sem("g_cleared")
        g_vec = sem("g_vec")
        g_tanh = sem("g_tanh")
        g_summed = sem("g_summed")
        g_scattered = sem("g_scattered")
        r_loaded = sem("r_loaded")
        r_turned = sem("r_turned")
        r_copied = sem("r_copied")
        r_summed = sem("r_summed")
        r_stored = sem("r_stored")
        h_turned = sem("h_turned")
        y_ready = sem("y_ready")
        norm = sem("norm")
        inverted = sem("inverted")
        std_ready = sem("std_ready")
        var_ready = sem("var_ready")
        out_ready = [sem(f"out_ready{n}") for n in range(NPIECE)]
        mean_scaled = sem("mean_scaled")
        centred = sem("centred")
        squared = sem("squared")
        out_stored = sem("out_stored")

        block = ctx.enter_context(nc.Block())

        NPARTS = -(-NQ // PARTS_OF)
        TABLES = NPARTS + 2

        def col(ap):
            return ap.rearrange("(a b) -> a b", b=1)

        def node_rows(ap, t):
            return ap[:, t].rearrange("p (t o) -> p t o", o=1).broadcast_to([NPART, PT, D])

        def divide(engine, n):
            t = slice(n * PT, (n + 1) * PT)
            engine.tensor_tensor(y2[:, t, :], y[:, t, :], node_rows(var, t), ALU.mult).then_inc(out_ready[n], 1)

        def row_use(i, k):
            return i * (SLOTS // RS) + k // RS

        def blocks(b):
            return range(b * BB, min(NBLK, (b + 1) * BB))

        def piece(n):
            return slice(n * PARTS_OF * BB * QB, min(NT, (n + 1) * PARTS_OF * BB * QB))

        @block.sync
        def _(sp):
            def edges(tile, array, loaded):
                sp.dma_start(tile[0:EFULL, 0:EW], array[0:EFULL * EW].rearrange("(p c) -> p c", c=EW)).then_inc(loaded, 16)
                sp.dma_start(tile[EFULL:EP, 0:EREST], array[EFULL * EW:E].rearrange("(p c) -> p c", p=1)).then_inc(loaded, 16)

            for n, (g, end) in enumerate(((0, 1), (1, SLOTS))):
                sp.dma_start(f_src[:, g:end, :].rearrange("p g (h c) -> p (g h) c", c=HC),
                             src[g * GE:end * GE].rearrange("(g p c) -> p g c", c=HC, p=P)).then_inc(first_loaded[n], 16)
            sp.wait_ge(e_set, 4)
            edges(e_dst, dst, dst_loaded)
            sp.dma_start(e_dst[0:EFULL, EW:EW + 1], col(dst[EW:EFULL * EW + 1:EW]),
                         allow_slow_non_contiguous=True).then_inc(dst_loaded, 16)
            for n, half in enumerate((slice(0, XSPLIT * QB * D), slice(XSPLIT * QB * D, NT * D))):
                sp.dma_start(xr[:, half], x.rearrange("(p t) d -> p (t d)", t=NT)[:, half]).then_inc(x_loaded[n], 16)
            edges(e_src, src, src_loaded)
            edges(e_typ, etype, typ_loaded)
            sp.dma_start(bases[:, 0:NHALF], dst[0:E:HE].rearrange("(p c) -> p c", p=1),
                         allow_slow_non_contiguous=True).then_inc(bases_loaded, 16)
            sp.wait_ge(e_row_made, 2 * GPP)
            sp.dma_start(row_dram.rearrange("(p a) e -> p (a e)", a=GPP), e_row16).then_inc(e_stored, 16)
            sp.wait_ge(last_made, 1)
            sp.wait_ge(e_cast, 1)
            sp.dma_start(meta_dram.rearrange("(p a) h q c -> p (a h q c)", a=GPP), e_meta.rearrange("p e c -> p (e c)")).then_inc(e_stored, 16)
            sp.wait_ge(e_cast, 2)
            sp.dma_start(typ_dram.rearrange("(p a) e -> p (a e)", a=GPP), e_typ16).then_inc(e_stored, 16)
            sp.wait_ge(bases_loaded, 16)
            sp.wait_ge(flag_set, 1)
            general = sp.value_load(flag[0:1, 0:1], min_val=0, max_val=2 * E)
            sp.wait_ge(e_stored, 48)

            def load_meta(g, k):
                sp.dma_start(f_meta[:, k].rearrange("p (h c) m -> p h (c m)", h=2), meta_dram[bass.ds(g, 1)].rearrange("a h p m -> (a p) h m")).then_inc(meta_loaded[k], 16)

            def load_rows(g, k):
                sp.dma_start(f_row[:, k, :], row_dram[bass.ds(g, 1), :].broadcast_to([P, GE])).then_inc(rows_loaded[k], 16)
                sp.dma_start(f_typ[:, k, :], typ_dram[bass.ds(g, 1), :].broadcast_to([R, GE])).then_inc(rows_loaded[k], 16)

            def load_q(g, k):
                for half in range(2):
                    base = sp.value_load(bases[0:1, bass.ds(2 * g + half, 1)], min_val=0, max_val=N - 1)
                    sp.dma_start(f_q[half * WIN:(half + 1) * WIN, k].rearrange("p a c -> p (a c)"), q_dram[bass.ds(base, WIN), :]).then_inc(rows_loaded[k], 16)

            with sp.If(general > 0):
                sp.wait_ge(tables, TABLES * 16)
                sp.dma_start(z_dram[0:P, :], zero[:, 0:UW]).then_inc(g_cleared, 16)
                for k in range(NZ - 1):
                    sp.dma_start(z_dram[P + k * ZB:P + (k + 1) * ZB, :].rearrange("(p r) c -> p (r c)", r=2), zero[0:GC, :]).then_inc(g_cleared, 16)
                sp.wait_ge(g_cleared, NZ * 16)
                with sp.Fori(0, GN) as i:
                    sp.dma_start(g_idx[:, 0:1], col(src[bass.ds(i * GC, GC)])).then_inc(g_loaded[0], 16)
                    sp.dma_start(g_idx[:, 1:2], col(dst[bass.ds(i * GC, GC)])).then_inc(g_loaded[1], 16)
                    sp.dma_start(g_idx[:, 2:3], col(etype[bass.ds(i * GC, GC)])).then_inc(g_loaded[2], 16)
                    sp.dma_start(g_row[:], dst[bass.ds(i * GC, GC)].rearrange("(a b) -> a b", a=1).broadcast_to([GC, GC])).then_inc(g_loaded[3], 16)
                    sp.wait_ge(g_scattered, i * 16 + 16).then_inc(sp_turn, 1)
                sp.dma_start(g_zrow, z_dram[0:GC, :]).then_inc(r_loaded, 16)
                with sp.Fori(1, NT) as t:
                    sp.wait_ge(r_turned, t).then_inc(sp_turn, 1)
                    sp.dma_start(g_zrow, z_dram[bass.ds(t * GC, GC), :]).then_inc(r_loaded, 16)
            with sp.Else():
                for k in range(SLOTS):
                    load_meta(k, k)
                for k in range(RS):
                    load_rows(k, k)
                sp.wait_ge(tables, TABLES * 16)
                for k in range(RS):
                    load_q(k, k)

                def turn(i, groups):
                    for k in range(groups):
                        g = i * SLOTS + k
                        sp.wait_ge(u_ready, i * (SLOTS * 2) + (k + 1 - SLOTS) * 2).then_inc(sp_turn, 1)
                        load_meta(g, k % SLOTS)
                        load_rows(g - RS, k % RS)
                        load_q(g - RS, k % RS)

                with sp.Fori(1, TURNS) as i:
                    turn(i, SLOTS)
                turn(TURNS, ENDG)
                for g in range(NG - RS, NG):
                    sp.wait_ge(u_ready, (g - RS + 1) * 2)
                    load_rows(g, g % RS)
                    load_q(g, g % RS)
            out_rows = out.rearrange("(p t) d -> p t d", t=NT)
            for n in range(NPIECE):
                sp.wait_ge(out_ready[n], 1)
                sp.dma_start(out_rows[:, n * PT:(n + 1) * PT, :], y2[:, n * PT:(n + 1) * PT, :]).then_inc(out_stored, 16)
            sp.wait_ge(out_stored, 16 * NPIECE)

        @block.gpsimd
        def _(pool):
            nc.gpsimd.memset(ident[:], 0.0).then_inc(pool_const, 1)
            nc.gpsimd.iota(iota_pi[:], pattern=[[0, 1]], base=0, channel_multiplier=1).then_inc(pool_const, 1)
            nc.gpsimd.iota(iota_ri[:], pattern=[[1, P]], base=0, channel_multiplier=0).then_inc(pool_const, 1)
            pool.wait_ge(pool_const, 1)
            nc.gpsimd.affine_select(out=ident[:], in_=ident[:], compare_op=ALU.not_equal, fill=1.0, base=0,
                                    pattern=[[-1, P]], channel_multiplier=1).then_inc(pool_const, 1)

            def gather(into, table, index):
                return nc.gpsimd.indirect_dma_start(into, None, table, bass.IndirectOffsetOnAxis(ap=index, axis=0))

            for g in range(SLOTS):
                pool.wait_ge(first_loaded[min(g, 1)], 16)
                for c in range(FC):
                    gather(f_x[:, g, c, 0:D], x, f_src[:, g, c:c + 1]).then_inc(gathered[g], 16)
            pool.wait_ge(flag_set, 1)
            general = pool.value_load(flag[0:1, 0:1], min_val=0, max_val=2 * E)

            with pool.If(general > 0):
                for g in range(SLOTS):
                    pool.wait_ge(gathered[g], 16 * FC)
                pool.wait_ge(g_cleared, NZ * 16)
                with pool.Fori(0, GN) as i:
                    for k in range(4):
                        pool.wait_ge(g_loaded[k], i * 16 + 16).then_inc(pool_turn, 1)
                    gather(g_x[:, 0:D], x, g_idx[:, 0:1]).then_inc(g_gathered[0], 16)
                    gather(g_q[:], q_dram, g_idx[:, 1:2]).then_inc(g_gathered[1], 16)
                    gather(g_rel[:], rel_dram, g_idx[:, 2:3]).then_inc(g_gathered[2], 16)
                    gather(g_z, z_dram, g_idx[:, 1:2]).then_inc(g_gathered[3], 16)
                    pool.wait_ge(g_vec, i * GV + GV).then_inc(pool_turn, 1)
                    nc.gpsimd.indirect_dma_start(z_dram, bass.IndirectOffsetOnAxis(ap=g_sidx[:], axis=0), g_new, None).then_inc(g_scattered, 16)
            with pool.Else():
                def turn(i, groups, end):
                    for k in range(groups):
                        slot, use = k % SLOTS, i + k // SLOTS
                        pool.wait_ge(meta_loaded[slot], use * 16 + 16).then_inc(pool_turn, 1)
                        for c in range(HC if end and k == groups - 1 else FC):
                            gather(f_x[:, slot, c, 0:D], x, f_meta[:, slot, c, 0:1]).then_inc(gathered[slot], 16)

                with pool.Fori(1, TURNS) as i:
                    turn(i, SLOTS, False)
                turn(TURNS, ENDG, True)

            def centre(n):
                t = slice(n * PT, (n + 1) * PT)
                pool.wait_ge(norm, n + 1)
                nc.gpsimd.tensor_scalar(mean[:, t], mean[:, t], 1.0 / D, None, ALU.mult).then_inc(mean_scaled, 1)
                pool.wait_ge(mean_scaled, n + 1)
                nc.gpsimd.tensor_tensor(y[:, t, :], y[:, t, :], node_rows(mean, t), ALU.subtract).then_inc(centred, 1)

            for n in range(NPIECE):
                centre(n)
                if n >= 3 and n - 3 not in DVE_DIVIDES:
                    pool.wait_ge(inverted, n - 2)
                    divide(nc.gpsimd, n - 3)

        @block.scalar
        def _(act):
            for tile, array in ((a1[:, 0:D], a1_w), (a1[:, D:D1], col(a1_b)), (a2[:, 0:D], a2_w), (a2[:, D:D1], col(a2_b)), (rel[:], rel_emb),
                                (relf[:, 0:NB], w_comp)):
                act.dma_start(tile, array).then_inc(a_loaded, 16)
            for tile, array in ((wf[:], weight.rearrange("(k b) i o -> (b i) k o", k=KB)), (ws[:], w_self)):
                act.dma_start(tile, array).then_inc(w_loaded, 16)
            act.wait_ge(dst_loaded, 48)
            for h in range(2 * GPP):
                act.wait_ge(e_shifted, h % 2 + 1)
                nc.scalar.activation(e_row16[:, h * HE:(h + 1) * HE], e_halves[:, h, :], ACT.Identity, bias=e_shift[:, h:h + 1]).then_inc(e_row_made, 1)
            for b in range(NQ):
                act.wait_ge(xT_turned, b + 1)
                if b >= QBUF:
                    act.wait_ge(q_made, b + 1 - QBUF)
                width = len(blocks(b)) * NPART
                nc.scalar.copy(xT[:, b % QBUF, 0:width], ps[b % QBUF][:, 0:width]).then_inc(xT_copied, 1)
            act.wait_ge(src_loaded, 32)
            nc.scalar.copy(e_meta[:, :, 0], e_src).then_inc(e_cast, 1)
            act.wait_ge(typ_loaded, 32)
            nc.scalar.copy(e_typ16, e_typ).then_inc(e_cast, 1)
            act.wait_ge(e_set, 6)
            act.dma_start(q_dram[N:ROWS, :], zero[:].bitcast(BF16)[:, 0:3 * D1]).then_inc(tables, 16)
            for part in range(3):
                for n in range(NPARTS):
                    if part == 0:
                        act.wait_ge(q_copied, min(NQ, (n + 1) * PARTS_OF))
                    else:
                        act.wait_ge(q_rest, (part - 1) * NPARTS + n + 1)
                    t = piece(n)
                    nc.scalar.copy(q3[:, t, part, :], (qf3, qr3, qf3)[part][:, t, :]).then_inc(q_part, 1)
                    if part == 2:
                        act.wait_ge(q_part, 2 * NPARTS + n + 1)
                        act.dma_start(q_dram[0:N, :].rearrange("(p t) c -> p t c", t=NT)[:, t, :],
                                      q3[:, t, :, :].rearrange("p t a c -> p t (a c)")).then_inc(tables, 16)
            act.wait_ge(split, 5)
            act.dma_start(rel_dram, rel3[:].rearrange("r a c -> r (a c)")).then_inc(tables, 16)
            act.wait_ge(e_stored, 48)
            nc.scalar.activation(accT[:, 0:CLEAR], zero[HP:HP + D, 0:1].broadcast_to([D, CLEAR]), ACT.Copy).then_inc(acc_clear, 1)
            act.wait_ge(flag_set, 1)
            general = act.value_load(flag[0:1, 0:1], min_val=0, max_val=2 * E)

            def tanh(g, k):
                act.wait_ge(score_ready, g + 1)
                nc.scalar.activation(f_th[:, k % 2, :], f_sc[:, k % 2, :], ACT.Tanh, scale=SCALE).then_inc(tanh_ready, 1)

            def last_flags(g, k, use, first):
                if not first:
                    act.wait_ge(u_ready, (g - 1) * 2)
                act.wait_ge(meta_loaded[k % SLOTS], use * 16 + 16)
                nc.scalar.copy(f_w[:, k % 2, :, NB], f_meta[:, k % SLOTS].bitcast(F32)[:, :, 1]).then_inc(last_ready, 1)

            def copy_s(g, k):
                act.wait_ge(s_turned, g + 1)
                for h in range(2):
                    last = nc.scalar.copy(f_s[:, k % 2, h * HC:(h + 1) * HC, :], s_ps[k % 2][h])
                last.then_inc(s_ready, 1)

            def copy_z(g, k, first):
                act.wait_ge(scattered, g + 1)
                if not first:
                    act.wait_ge(zt_turned, g)
                for h in range(2):
                    nc.scalar.copy(f_zs[:, h * HALF:(h + 1) * HALF], z_ps[k % 2][h][:, 0:HALF]).then_inc(z_copied, 1)

            def copy_zt(g, first):
                act.wait_ge(zt_turned, g + 1)
                if not first:
                    act.wait_ge(h_summed, g)
                nc.scalar.copy(f_zts[:, 0:KB, :].rearrange("p k n -> p (k n)"), zt_ps[:]).then_inc(zt_copied, 1)
                nc.scalar.copy(f_zts[0:D, KB, :], zl_ps).then_inc(zt_copied, 1)

            def root(n):
                act.wait_ge(var_ready, n + 1)
                t = slice(n * PT, (n + 1) * PT)
                nc.scalar.activation(mean[:, t], var[:, t], ACT.Sqrt, bias=eps[0:NPART, 0:1], scale=1.0 / D).then_inc(std_ready, 1)

            with act.If(general > 0):
                with act.Fori(0, GN) as i:
                    act.wait_ge(g_vec, i * GV + 8)
                    nc.scalar.activation(g_sc[:, 1:2], g_sc[:, 0:1], ACT.Tanh, scale=SCALE).then_inc(g_tanh, 1)
                with act.Fori(0, NT) as t:
                    act.wait_ge(r_turned, t + 1)
                    nc.scalar.copy(f_zts[:, 0:KB, 0:GC], ps[0][:, 0:KB * GC].rearrange("p (k n) -> p k n", k=KB)).then_inc(r_copied, 1)
                    nc.scalar.copy(f_zts[0:D, KB, 0:GC], ps[1][0:D, 0:GC]).then_inc(r_copied, 1)
                act.nop()
            with act.Else():
                def turn(i, groups, peel, end):
                    for k in range(groups):
                        g = i * SLOTS + k
                        last_flags(g, k, i + k // SLOTS, peel and k < 2)
                        tanh(g, k)
                        if not (peel and k == 0):
                            copy_z(g - 1, k - 1, peel and k == 1)
                        if not (end and k == groups - 1):
                            copy_s(g + 1, k + 1)
                        if not (peel and k == 0):
                            copy_zt(g - 1, peel and k == 1)
                copy_s(0, 0)
                turn(0, SLOTS, True, False)
                with act.Fori(1, TURNS) as i:
                    turn(i, SLOTS, False, False)
                turn(TURNS, ENDG, False, True)
                copy_z(NG - 1, ENDG - 1, False)
                copy_zt(NG - 1, False)
            nc.scalar.activation(root_early[:], eps[:], ACT.Sqrt)
            for n in range(NPIECE):
                t = slice(n * PT, (n + 1) * PT)
                act.wait_ge(centred, n + 1)
                nc.scalar.activation(y2[:, t, :], y[:, t, :], ACT.Square).then_inc(squared, 1)
                if n:
                    root(n - 1)
            root(NPIECE - 1)

        @block.tensor
        def _(pe):
            pe.wait_ge(pool_const, 4)
            pe.wait_ge(a_loaded, 96)
            nc.tensor.transpose(ps[4][0:D, 0:R], rel[:], ident[0:R, 0:R]).then_inc(small_mm, 1)
            for j in range(QB):
                nc.tensor.matmul(ps[5][j * D:(j + 1) * D, j * D1:(j + 1) * D1], a2[:, 0:D], a1[:], start=True, stop=True).then_inc(small_mm, 1)
            pe.wait_ge(small_copied, 2)
            nc.tensor.matmul(ps[6][0:R, 0:D1], relT[:], a1[:], start=True, stop=True).then_inc(small_mm, 1)
            nc.tensor.matmul(ps[7][0:NPART, 0:D1], a2_bias[:], a1[:], start=True, stop=True).then_inc(small_mm, 1)

            def turn_x(b):
                for n in range(1 if blocks(b)[-1] < XSPLIT else 2):
                    pe.wait_ge(x_loaded[n], 16)
                if b >= QBUF:
                    pe.wait_ge(xT_copied, b + 1 - QBUF)
                for j in blocks(b):
                    last = nc.tensor.transpose(ps[b % QBUF][:, (j - b * BB) * NPART:(j - b * BB + 1) * NPART],
                                               xr[:, j * QB * D:(j + 1) * QB * D], ident[0:NPART, 0:NPART])
                last.then_inc(xT_turned, 1)

            def make_q(b):
                pe.wait_ge(xT_copied, b + 1)
                if b >= QBANK:
                    pe.wait_ge(q_copied, b + 1 - QBANK)
                for j in range(len(blocks(b))):
                    last = nc.tensor.matmul(ps[QBUF + b % QBANK][0:NPART, j * QW:(j + 1) * QW], xT[:, b % QBUF, j * NPART:(j + 1) * NPART],
                                            bblock[:], start=True, stop=True)
                last.then_inc(q_made, 1)

            turn_x(0)
            turn_x(1)
            for b in range(NQ):
                if b + 2 < NQ:
                    turn_x(b + 2)
                if b == 0:
                    pe.wait_ge(small_copied, 4 + QB)
                make_q(b)
            pe.wait_ge(w_loaded, 32)
            pe.wait_ge(e_checked, 5)
            nc.tensor.matmul(ps[7][0:1, 0:2 * GPP + 1], ones[0:EP, :], e_count[:], start=True, stop=True).then_inc(small_mm, 1)
            pe.wait_ge(flag_set, 1)
            general = pe.value_load(flag[0:1, 0:1], min_val=0, max_val=2 * E)

            def chunk(tile, k, c):
                first = (c // HC) * HE + c % HC
                return tile[:, k % 2, first:(c // HC + 1) * HE:HC]

            def add_vq(g, k, use):
                pe.wait_ge(onehots, g + 1)
                pe.wait_ge(rows_loaded[k % RS], use * 64 + 64)
                for c in range(FC):
                    out_c = vq_ps[k % 2][:, c, :]
                    for a in range(3):
                        nc.tensor.matmul(out_c, chunk(f_rT, k, c), rel3[:, a, :], start=(a == 0), stop=False)
                    for a in range(3):
                        last = nc.tensor.matmul(out_c[:, NB:CK], chunk(f_dT, k, c), f_q[:, k % RS, a, :], start=False, stop=(a == 2))
                last.then_inc(vq_ready, 1)

            def turn_s(g, k):
                for c in range(FC):
                    w = (c // HC) * WIN
                    last = nc.tensor.transpose(s_ps[k % 2][c // HC][:, c % HC, :], chunk(f_dT, k, c)[w:w + WIN, :], ident16[w:w + WIN, w:w + WIN])
                last.then_inc(s_turned, 1)

            def scatter(g, k, pair, halves=2):
                if pair == 0:
                    pe.wait_ge(s_ready, g + 1)
                    pe.wait_ge(u_ready, g * 2 + 1)
                if pair == 1:
                    pe.wait_ge(u_ready, g * 2 + 2)
                for h in range(2):
                    for c in (pair, pair + HC)[0:halves]:
                        w = (c // HC) * WIN
                        last = nc.tensor.matmul(z_ps[k % 2][h][w:w + WIN, 0:HALF], f_s[:, k % 2, c, :], fu2[:, k % 2, c, h * HALF:(h + 1) * HALF],
                                                start=(pair == 0), stop=(pair == HC - 1))
                if pair == HC - 1:
                    last.then_inc(scattered, 1)

            def turn_z(g, first):
                pe.wait_ge(z_copied, g * 2 + 2)
                if not first:
                    pe.wait_ge(zt_copied, g * 2)
                for b in range(KB):
                    nc.tensor.transpose(zt_ps[:, b * P:(b + 1) * P], f_zs[:, b * P:(b + 1) * P], ident[:])
                nc.tensor.transpose(zl_ps, f_zs[:, KB * P:UW], ident[:]).then_inc(zt_turned, 1)

            def weigh(g, first):
                pe.wait_ge(zt_copied, g * 2 + 2)
                if not first:
                    pe.wait_ge(h_added, 2 * g)
                for b in range(KB):
                    nc.tensor.matmul(h_ps, wf[:, b, :], f_zts[:, b, :], start=(b == 0), stop=False)
                nc.tensor.matmul(h_ps, ws[:], f_zts[0:D, KB, :], start=False, stop=True).then_inc(h_summed, 1)

            with pe.If(general > 0):
                with pe.Fori(0, GN) as i:
                    pe.wait_ge(g_vec, i * GV + 15)
                    for h in range(2):
                        last = nc.tensor.matmul(ps[h][0:GC, 0:HALF], g_same, g_u[:, h * HALF:(h + 1) * HALF], start=True, stop=True)
                    last.then_inc(g_summed, 1)
                with pe.Fori(0, NT) as t:
                    pe.wait_ge(r_loaded, t * 16 + 16)
                    for b in range(KB):
                        nc.tensor.transpose(ps[0][:, b * GC:(b + 1) * GC], g_zrow[:, b * P:(b + 1) * P], ident[0:GC, 0:GC])
                    nc.tensor.transpose(ps[1][0:D, 0:GC], g_zrow[:, KB * P:UW], ident[0:GC, 0:GC]).then_inc(r_turned, 1)
                    pe.wait_ge(r_copied, t * 2 + 2)
                    for b in range(KB):
                        nc.tensor.matmul(ps[2][HP:HP + D, 0:GC], wf[:, b, :], f_zts[:, b, 0:GC], start=(b == 0), stop=False)
                    nc.tensor.matmul(ps[2][HP:HP + D, 0:GC], ws[:], f_zts[0:D, KB, 0:GC], start=False, stop=True).then_inc(r_summed, 1)
                    pe.wait_ge(r_stored, t + 1)
                pe.nop()
            with pe.Else():
                def turn(i, groups, peel, end):
                    for k in range(groups):
                        g = i * SLOTS + k
                        halves = 1 if end and k == groups - 1 else 2
                        scatter(g, k, 0, halves)
                        if not (peel and k == 0):
                            turn_z(g - 1, peel and k == 1)
                        if not (end and k == groups - 1):
                            turn_s(g + 1, k + 1)
                        if not (end and k >= groups - 2):
                            add_vq(g + 2, k + 2, row_use(i, k + 2))
                        scatter(g, k, 1, halves)
                        if not (peel and k == 0):
                            weigh(g - 1, peel and k == 1)
                        scatter(g, k, 2, halves)
                add_vq(0, 0, 0)
                turn_s(0, 0)
                add_vq(1, 1, 0)
                turn(0, SLOTS, True, False)
                with pe.Fori(1, TURNS) as i:
                    turn(i, SLOTS, False, False)
                turn(TURNS, ENDG, False, True)
                turn_z(NG - 1, False)
                weigh(NG - 1, False)
                pe.wait_ge(h_added, NHALF)
                pe.nop()
            for b in range(NH):
                if b >= 6:
                    pe.wait_ge(y_ready, b - 5)
                for j in range(HB):
                    t = b * HB + j
                    last = nc.tensor.transpose(ps[b % 6][0:NPART, j * D:(j + 1) * D], accT[:, t:N:NT], ident[HP:HP + D, HP:HP + D])
                last.then_inc(h_turned, 1)

        @block.vector
        def _(dve):
            for tile, value, first in ((e_dst, FAR, EREST), (e_src, 0, EREST), (e_typ, NOREL, EREST)):
                nc.vector.memset(tile[EQ:EP, first:], value).then_inc(e_set, 1)
            nc.vector.memset(bases[:], 0).then_inc(e_set, 1)
            nc.vector.memset(bblock[:], 0.0).then_inc(const, 1)
            nc.vector.memset(g_x[:, D:D1], 1.0).then_inc(const, 1)
            nc.vector.memset(ones[:], 1.0).then_inc(const, 1)
            nc.vector.memset(eps[:], EPS).then_inc(e_set, 1)
            nc.vector.memset(f_x[:, :, :, D], 1.0).then_inc(const, 1)
            nc.vector.memset(zero[:], 0.0).then_inc(e_set, 1)
            dve.wait_ge(dst_loaded, 48)
            firsts = e_halves[:, :, 0].rearrange("p (a h) -> p a h", h=2)
            shifts = e_shift[:].rearrange("p (a h) -> p a h", h=2)
            for h in range(2):
                nc.vector.tensor_scalar(shifts[:, :, h], firsts[:, :, h], -1.0, float(h * WIN), ALU.mult, ALU.add).then_inc(e_shifted, 1)
            nc.vector.tensor_tensor(e_metaf[:, :, 1], e_dst[:, 0:EW], e_dst[:, 1:EW + 1], ALU.not_equal).then_inc(last_made, 1)
            dve.wait_ge(a_loaded, 96)
            nc.vector.tensor_copy(a2_bias[:], a2[:, D:D1].broadcast_to([D, NPART])).then_inc(small_copied, 1)
            dve.wait_ge(small_mm, 1)
            nc.vector.tensor_copy(relT[:], ps[4][0:D, 0:R]).then_inc(small_copied, 1)
            dve.wait_ge(const, 1)
            for j in range(QB):
                dve.wait_ge(small_mm, j + 2)
                nc.vector.tensor_copy(bblock[j * D:(j + 1) * D, j * D1:(j + 1) * D1], ps[5][j * D:(j + 1) * D, j * D1:(j + 1) * D1]).then_inc(small_copied, 1)
            dve.wait_ge(small_mm, QB + 2)
            nc.vector.tensor_copy(relf[:, NB:CK], ps[6][0:R, 0:D1]).then_inc(small_copied, 1)
            dve.wait_ge(small_mm, QB + 3)
            nc.vector.tensor_copy(q_bias[:], ps[7][0:NPART, 0:D1]).then_inc(small_copied, 1)
            nc.vector.tensor_tensor(e_down, e_dst[:, 0:EW], e_dst[:, 1:EW + 1], ALU.is_gt).then_inc(e_checked, 1)

            def copy_q(b):
                dve.wait_ge(q_made, b + 1)
                tiles = len(blocks(b)) * QB
                nc.vector.tensor_tensor(qf3[:, b * BB * QB:b * BB * QB + tiles, :],
                                        ps[QBUF + b % QBANK][0:NPART, 0:tiles * D1].rearrange("p (t c) -> p t c", c=D1),
                                        q_bias[:].rearrange("p (o c) -> p o c", o=1).broadcast_to([NPART, tiles, D1]), ALU.add).then_inc(q_copied, 1)

            for b in range(0, PARTS_OF):
                copy_q(b)
            dve.wait_ge(e_checked, 1)
            nc.vector.tensor_reduce(e_count[:, 2 * GPP:2 * GPP + 1], e_down, AX_X, ALU.add).then_inc(e_checked, 1)
            for b in range(PARTS_OF, 2 * PARTS_OF):
                copy_q(b)
            nc.vector.tensor_reduce(e_count[:, 0:2 * GPP], e_halves, AX_X, ALU.max).then_inc(e_checked, 1)
            dve.wait_ge(e_checked, 3)
            nc.vector.tensor_tensor(e_count[:, 0:2 * GPP], e_count[:, 0:2 * GPP], e_halves[:, :, 0], ALU.subtract).then_inc(e_checked, 1)
            dve.wait_ge(e_checked, 4)
            nc.vector.tensor_scalar(e_count[:, 0:2 * GPP], e_count[:, 0:2 * GPP], float(WIN), None, ALU.is_ge).then_inc(e_checked, 1)
            for b in range(2 * PARTS_OF, NQ):
                copy_q(b)
            dve.wait_ge(small_copied, QB + 3)
            nc.vector.tensor_copy(rel3[:, 0, :], relf[:]).then_inc(split, 1)
            dve.wait_ge(split, 1)
            nc.vector.tensor_tensor(relr[:], relf[:], rel3[:, 0, :], ALU.subtract).then_inc(split, 1)
            dve.wait_ge(split, 2)
            nc.vector.tensor_copy(rel3[:, 1, :], relr[:]).then_inc(split, 1)
            dve.wait_ge(split, 3)
            nc.vector.tensor_tensor(relf[:], relr[:], rel3[:, 1, :], ALU.subtract).then_inc(split, 1)
            dve.wait_ge(split, 4)
            nc.vector.tensor_copy(rel3[:, 2, :], relf[:]).then_inc(split, 1)
            for part in range(2):
                for n in range(NPARTS):
                    dve.wait_ge(q_part, part * NPARTS + n + 1)
                    full, rest = ((qf3, qr3), (qr3, qf3))[part]
                    nc.vector.tensor_tensor(rest[:, piece(n), :], full[:, piece(n), :], q3[:, piece(n), part, :], ALU.subtract).then_inc(q_rest, 1)
                if part == 0:
                    dve.wait_ge(small_mm, QB + 4)
                    nc.vector.tensor_reduce(e_total[:], ps[7][0:1, 0:2 * GPP + 1], AX_X, ALU.add).then_inc(e_checked, 1)
                    dve.wait_ge(e_checked, 6)
                    nc.vector.tensor_scalar(flag[:], e_total[:], -1.0, None, ALU.add).then_inc(flag_set, 1)
            dve.wait_ge(pool_const, 4)
            nc.vector.tensor_copy(iota_p[:], iota_pi[:]).then_inc(const, 1)
            nc.vector.tensor_copy(iota_r[:], iota_ri[:]).then_inc(const, 1)
            nc.vector.tensor_copy(ident16[:], ident[:]).then_inc(const, 1)
            dve.wait_ge(const, 7)
            nc.vector.tensor_scalar(upper[:], iota_r[:], iota_p[:, 0:1], None, ALU.is_gt).then_inc(const, 1)
            nc.vector.tensor_scalar(spare_row[:], iota_p[:], float(N), None, ALU.add).then_inc(const, 1)
            dve.wait_ge(e_stored, 48)
            nc.vector.memset(accT[:, CLEAR:], 0.0).then_inc(acc_clear, 1)
            dve.wait_ge(acc_clear, 2)
            dve.wait_ge(const, 9)
            dve.wait_ge(bases_loaded, 16)
            dve.wait_ge(flag_set, 1)
            general = dve.value_load(flag[0:1, 0:1], min_val=0, max_val=2 * E)

            def one_hot_rows(g, k, use, first):
                dve.wait_ge(rows_loaded[k % RS], use * 64 + 64)
                if not first:
                    dve.wait_ge(s_turned, g - 1)
                nc.vector.tensor_scalar(f_dT[:, k % 2, :], f_row[:, k % RS, :], iota_p[:, 0:1], None, ALU.is_equal)

            def one_hot_relations(g, k):
                nc.vector.tensor_scalar(f_rT[:, k % 2, :], f_typ[:, k % RS, :], iota_p[0:R, 0:1], None, ALU.is_equal).then_inc(onehots, 1)

            def score(g, k, use, use_ahead, halves):
                dve.wait_ge(vq_ready, g + 1)
                dve.wait_ge(gathered[k % SLOTS], use * 16 * FC + 16 * HC * halves)
                nc.vector.tensor_tensor(f_prod[:], vq_ps[k % 2][:, :, NB:CK], f_x[:, k % SLOTS], ALU.mult).then_inc(prod_ready, 1)
                if use_ahead is not None:
                    one_hot_rows(g + 2, k + 2, use_ahead, False)
                dve.wait_ge(prod_ready, g + 1)
                nc.vector.tensor_reduce(f_sc[:, k % 2, :], f_prod[:], AX_X, ALU.add).then_inc(score_ready, 1)
                if use_ahead is not None:
                    one_hot_relations(g + 2, k + 2)

            def weights(g, k):
                dve.wait_ge(tanh_ready, g + 1)
                nc.vector.scalar_tensor_tensor(out=f_w[:, k % 2, :, 0:NB], in0=f_th[:, k % 2, :].rearrange("p (c o) -> p c o", o=1).broadcast_to([P, FC, NB]),
                                               scalar=0.0, in1=vq_ps[k % 2][:, :, 0:NB], op0=ALU.max, op1=ALU.mult).then_inc(w_ready, 1)

            def spread(g, k, first, pairs, halves):
                if pairs[0] == 0:
                    dve.wait_ge(w_ready, g + 1)
                    dve.wait_ge(last_ready, g + 1)
                    if not first:
                        dve.wait_ge(scattered, g - 1)
                for pair in pairs:
                    chunks = slice(pair, HC * halves, HC)
                    last = nc.vector.tensor_tensor(fu[:, k % 2, chunks],
                                                   f_w[:, k % 2, chunks, :].rearrange("p c (b o) -> p c b o", o=1).broadcast_to([P, halves, NB + 1, D]),
                                                   f_x[:, k % SLOTS, chunks, 0:D].rearrange("p c (o d) -> p c o d", o=1).broadcast_to([P, halves, NB + 1, D]), ALU.mult)
                last.then_inc(u_ready, 1)

            def window_bases(g):
                return [dve.value_load(bases[0:1, bass.ds(2 * g + half, 1)], min_val=0, max_val=N - 1) for half in range(2)]

            def add_h(g, base, half, first):
                window = accT[:, bass.ds(base[half], WIN)]
                if half == 0:
                    dve.wait_ge(h_summed, g + 1)
                if half or not first:
                    dve.wait_ge(h_added, 2 * g + half)
                nc.vector.tensor_tensor(window, window, h_ps[:, half * WIN:(half + 1) * WIN], ALU.add).then_inc(h_added, 1)

            with dve.If(general > 0):
                with dve.Fori(0, GN) as i:
                    for k in range(4):
                        dve.wait_ge(g_gathered[k], i * 16 + 16)
                    nc.vector.tensor_tensor(g_v[:], g_q[:, 0:D1], g_q[:, D1:2 * D1], ALU.add).then_inc(g_vec, 1)
                    dve.wait_ge(g_vec, i * GV + 1)
                    nc.vector.tensor_tensor(g_v[:], g_v[:], g_q[:, 2 * D1:3 * D1], ALU.add).then_inc(g_vec, 1)
                    nc.vector.tensor_tensor(g_c[:], g_rel[:, 0:CK], g_rel[:, CK:2 * CK], ALU.add).then_inc(g_vec, 1)
                    dve.wait_ge(g_vec, i * GV + 3)
                    nc.vector.tensor_tensor(g_c[:], g_c[:], g_rel[:, 2 * CK:3 * CK], ALU.add).then_inc(g_vec, 1)
                    dve.wait_ge(g_vec, i * GV + 4)
                    nc.vector.tensor_tensor(g_v[:], g_v[:], g_c[:, NB:CK], ALU.add).then_inc(g_vec, 1)
                    nc.vector.tensor_copy(g_sc[:, 2:3], g_idx[:, 1:2]).then_inc(g_vec, 1)
                    dve.wait_ge(g_vec, i * GV + 6)
                    nc.vector.tensor_tensor(g_v[:], g_v[:], g_x[:], ALU.mult).then_inc(g_vec, 1)
                    dve.wait_ge(g_vec, i * GV + 7)
                    nc.vector.tensor_reduce(g_sc[:, 0:1], g_v[:], AX_X, ALU.add).then_inc(g_vec, 1)
                    nc.vector.tensor_scalar(g_same, g_row[:], g_sc[:, 2:3], None, ALU.is_equal).then_inc(g_vec, 1)
                    dve.wait_ge(g_vec, i * GV + 9)
                    nc.vector.tensor_tensor(g_later, g_same, upper[0:GC, 0:GC], ALU.mult).then_inc(g_vec, 1)
                    dve.wait_ge(g_vec, i * GV + 10)
                    nc.vector.tensor_reduce(g_sc[:, 3:4], g_later, AX_X, ALU.add).then_inc(g_vec, 1)
                    dve.wait_ge(g_vec, i * GV + 11)
                    nc.vector.tensor_scalar(g_w[:, NB:NB + 1], g_sc[:, 3:4], 0.0, None, ALU.is_equal).then_inc(g_vec, 1)
                    dve.wait_ge(g_tanh, i + 1)
                    nc.vector.scalar_tensor_tensor(out=g_w[:, 0:NB], in0=g_sc[:, 1:2].broadcast_to([GC, NB]), scalar=0.0, in1=g_c[:, 0:NB],
                                                   op0=ALU.max, op1=ALU.mult).then_inc(g_vec, 1)
                    dve.wait_ge(g_vec, i * GV + 13)
                    nc.vector.tensor_scalar(g_sc[:, 2:3], g_sc[:, 2:3], spare_row[0:GC, 0:1], g_w[:, NB:NB + 1], ALU.subtract, ALU.mult).then_inc(g_vec, 1)
                    nc.vector.tensor_tensor(g_u.rearrange("p (b d) -> p b d", d=D),
                                            g_w[:].rearrange("p (b o) -> p b o", o=1).broadcast_to([GC, NB + 1, D]),
                                            g_x[:, 0:D].rearrange("p (o d) -> p o d", o=1).broadcast_to([GC, NB + 1, D]), ALU.mult).then_inc(g_vec, 1)
                    dve.wait_ge(g_vec, i * GV + 15)
                    nc.vector.tensor_scalar(g_sidx[:], g_sc[:, 2:3], spare_row[0:GC, 0:1], None, ALU.add).then_inc(g_vec, 1)
                    dve.wait_ge(g_summed, i + 1)
                    nc.vector.tensor_tensor(g_new[:, 0:HALF], ps[0][0:GC, 0:HALF], g_z[:, 0:HALF], ALU.add)
                    nc.vector.tensor_tensor(g_new[:, HALF:NB * D], ps[1][0:GC, 0:NB * D - HALF], g_z[:, HALF:NB * D], ALU.add)
                    nc.vector.tensor_copy(g_new[:, NB * D:UW], ps[1][0:GC, NB * D - HALF:HALF]).then_inc(g_vec, 1)
                with dve.Fori(0, NT) as t:
                    dve.wait_ge(r_summed, t + 1)
                    nc.vector.tensor_copy(accT[:, bass.ds(t * GC, GC)], ps[2][HP:HP + D, 0:GC]).then_inc(r_stored, 1)
            with dve.Else():
                def turn(i, groups, peel, end):
                    for k in range(groups):
                        g = i * SLOTS + k
                        halves = 1 if end and k == groups - 1 else 2
                        if not (peel and k < 2):
                            base = window_bases(g - 2)
                        score(g, k, i + k // SLOTS, None if end and k >= groups - 2 else row_use(i, k + 2), halves)
                        weights(g, k)
                        for half, pairs in ((0, (0,)), (1, (1, 2))):
                            if not (peel and k < 2):
                                add_h(g - 2, base, half, peel and k == 2)
                            spread(g, k, peel and k < 2, pairs, halves)

                for k in range(2):
                    one_hot_rows(k, k, 0, True)
                    one_hot_relations(k, k)
                turn(0, SLOTS, True, False)
                with dve.Fori(1, TURNS) as i:
                    turn(i, SLOTS, False, False)
                turn(TURNS, ENDG, False, True)
                ends = [(g, window_bases(g)) for g in (NG - 2, NG - 1)]
                for g, base in ends:
                    for half in range(min(2, NHALF - 2 * g)):
                        add_h(g, base, half, False)
            def add_x(n):
                t = slice(n * PT, (n + 1) * PT)
                for b in range(n * PT // HB, (n + 1) * PT // HB):
                    dve.wait_ge(h_turned, b + 1)
                    nc.vector.scalar_tensor_tensor(out=qf[:, b * HB * D:(b + 1) * HB * D], in0=ps[b % 6][0:NPART, 0:HB * D],
                                                   scalar=0.0, in1=xr[:, b * HB * D:(b + 1) * HB * D], op0=ALU.max, op1=ALU.add).then_inc(y_ready, 1)
                dve.wait_ge(y_ready, (n + 1) * PT // HB)
                nc.vector.tensor_reduce(mean[:, t], y[:, t, :], AX_X, ALU.add).then_inc(norm, 1)

            def variance(n):
                t = slice(n * PT, (n + 1) * PT)
                dve.wait_ge(squared, n + 1)
                nc.vector.tensor_reduce(var[:, t], y2[:, t, :], AX_X, ALU.add).then_inc(var_ready, 1)

            def invert(n):
                dve.wait_ge(std_ready, n + 1)
                t = slice(n * PT, (n + 1) * PT)
                nc.vector.reciprocal(var[:, t], mean[:, t]).then_inc(inverted, 1)

            def finish(n):
                invert(n)
                if n in DVE_DIVIDES:
                    dve.wait_ge(inverted, n + 1)
                    divide(nc.vector, n)

            for n in range(NPIECE):
                add_x(n)
                if n >= 2:
                    variance(n - 2)
                if n >= 3:
                    finish(n - 3)
            for n in range(NPIECE - 2, NPIECE):
                variance(n)
                finish(n - 1)
            finish(NPIECE - 1)


_INS = ["x", "src", "dst", "edge_type_86", "L0_gnn_weight", "L0_gnn_w_comp", "L0_gnn_self_loop_weight",
        "L0_gnn_A1_w", "L0_gnn_A1_b", "L0_gnn_A2_w", "L0_gnn_A2_b", "L0_gnn_rel_emb"]


def kernel(**inputs):
    import numpy as _np
    import concourse.bacc as _bacc
    from concourse import mybir as _mybir
    from concourse.bass_utils import run_bass_kernel_spmd as _run

    nc = _bacc.Bacc("TRN2", target_bir_lowering=False, num_devices=1)
    arrays, args = {}, []
    for name in _INS:
        a = _np.ascontiguousarray(inputs[name])
        arrays[f"in_{name}"] = a
        args.append(nc.dram_tensor(f"in_{name}", a.shape, _mybir.dt.from_np(a.dtype), kind="ExternalInput").ap())
    out = nc.dram_tensor("out", args[0].shape, F32, kind="ExternalOutput").ap()
    build(nc, *args, out)
    r = _run(nc, [arrays], core_ids=[0])
    return r.results[0]["out"]
```
